# Optimizing a Trainium2 kernel written in Bass

```python
import numpy as np
import jax
import jax.numpy as jnp

def _softmax(x, axis=-1):
    return jax.nn.softmax(x, axis=axis)

def _gelu(x):
    return jax.nn.gelu(x, approximate=True)

def _silu(x):
    return jax.nn.silu(x)

def _sigmoid(x):
    return jax.nn.sigmoid(x)

def _layernorm(x, axis=-1, eps=1e-05):
    m = jnp.mean(x, axis=axis, keepdims=True)
    v = jnp.var(x, axis=axis, keepdims=True)
    return (x - m) / jnp.sqrt(v + eps)

def _scatter_add(tgt, idx, src, axis=0):
    return tgt.at[idx].add(src)

def _segment_sum(src, seg, n):
    return jax.ops.segment_sum(src, seg, n)
kernel_name = 'mk_seq_postln_d1_jaxref_r8_cbc7de'

def setup_inputs(seed: int=0):
    np.random.seed(seed)
    _w = jnp.asarray

    def _L0_attn_setup():
        import jax, jax.numpy as jnp
        import numpy as np
        NUM_HEADS = 16
        WINDOW = 16

        def sliding_mask(seq_len):
            i = jnp.arange(seq_len)[:, None]
            j = jnp.arange(seq_len)[None, :]
            return jnp.where(jnp.abs(i - j) <= WINDOW // 2, 0.0, -jnp.inf).astype(jnp.float32)
        key = jax.random.key(seed)
        k1, k2, k3 = jax.random.split(key, 3)
        B, S, D = (2, 256, 128)
        scale = 1.0 / np.sqrt(D)
        return {'input_embeddings': jax.random.normal(k1, (B, S, D), dtype=jnp.float32), 'token_ids': jax.random.randint(k2, (B, S), 0, 4000, dtype=jnp.int64), 'w_qkv': jax.random.normal(jax.random.fold_in(k3, 0), (3 * D, D), dtype=jnp.float32) * scale, 'b_qkv': jnp.zeros((3 * D,), dtype=jnp.float32), 'w_out': jax.random.normal(jax.random.fold_in(k3, 1), (D, D), dtype=jnp.float32) * scale, 'b_out': jnp.zeros((D,), dtype=jnp.float32)}
    _L0_attn_in = _L0_attn_setup()

    def _L0_ffn_setup():
        import jax, jax.numpy as jnp
        import numpy as np
        TOP_K = 32
        TEMPERATURE = 1.0
        PARAM_SCALE = 0.02

        def _compose_weight(logits, A, B):
            vals, idx = jax.lax.top_k(logits, TOP_K)
            w = jax.nn.softmax(vals / TEMPERATURE)
            A_sel = A[idx]
            B_sel = B[idx]
            return jnp.einsum('k,kir,kro->io', w, A_sel, B_sel)
        key = jax.random.key(seed)
        ks = jax.random.split(key, 7)
        B, S, D, F, P, R = (2, 128, 128, 512, 32, 64)
        x = jax.random.normal(ks[0], (B, S, D), dtype=jnp.float32)
        fc1_A = jax.random.normal(ks[1], (P, D, R), dtype=jnp.float32) * PARAM_SCALE
        fc1_B = jax.random.normal(ks[2], (P, R, F), dtype=jnp.float32) * PARAM_SCALE
        fc2_A = jax.random.normal(ks[3], (P, F, R), dtype=jnp.float32) * PARAM_SCALE
        fc2_B = jax.random.normal(ks[4], (P, R, D), dtype=jnp.float32) * PARAM_SCALE
        fc1_logits = jax.random.normal(ks[5], (P,), dtype=jnp.float32)
        fc2_logits = jax.random.normal(ks[6], (P,), dtype=jnp.float32)
        return {'x': x, 'fc1_A': fc1_A, 'fc1_B': fc1_B, 'fc2_A': fc2_A, 'fc2_B': fc2_B, 'fc1_logits': fc1_logits, 'fc2_logits': fc2_logits}
    _L0_ffn_in = _L0_ffn_setup()
    _d = {'L0_attn_input_embeddings': _L0_attn_in['input_embeddings'], 'L0_attn_token_ids': _L0_attn_in['token_ids'], 'L0_attn_w_qkv': _L0_attn_in['w_qkv'], 'L0_attn_b_qkv': _L0_attn_in['b_qkv'], 'L0_attn_w_out': _L0_attn_in['w_out'], 'L0_attn_b_out': _L0_attn_in['b_out'], 'L0_ffn_fc1_A': _L0_ffn_in['fc1_A'], 'L0_ffn_fc1_B': _L0_ffn_in['fc1_B'], 'L0_ffn_fc2_A': _L0_ffn_in['fc2_A'], 'L0_ffn_fc2_B': _L0_ffn_in['fc2_B'], 'L0_ffn_fc1_logits': _L0_ffn_in['fc1_logits'], 'L0_ffn_fc2_logits': _L0_ffn_in['fc2_logits']}
    _x0 = _d['L0_attn_input_embeddings']
    _d['L0_attn_input_embeddings'] = jax.random.normal(jax.random.fold_in(jax.random.key(seed), 1), (8, 256, 128), dtype=_x0.dtype)
    del _x0
    return _d

def reference(L0_attn_input_embeddings, L0_attn_token_ids, L0_attn_w_qkv, L0_attn_b_qkv, L0_attn_w_out, L0_attn_b_out, L0_ffn_fc1_A, L0_ffn_fc1_B, L0_ffn_fc2_A, L0_ffn_fc2_B, L0_ffn_fc1_logits, L0_ffn_fc2_logits):

    def _L0_attn_ref(input_embeddings, token_ids, w_qkv, b_qkv, w_out, b_out):
        import jax, jax.numpy as jnp
        import numpy as np
        NUM_HEADS = 16
        WINDOW = 16

        def sliding_mask(seq_len):
            i = jnp.arange(seq_len)[:, None]
            j = jnp.arange(seq_len)[None, :]
            return jnp.where(jnp.abs(i - j) <= WINDOW // 2, 0.0, -jnp.inf).astype(jnp.float32)
        B, S, D = input_embeddings.shape
        H = NUM_HEADS
        hd = D // H
        qkv = input_embeddings @ w_qkv.T + b_qkv
        q, k, v = jnp.split(qkv, 3, axis=-1)
        q = q.reshape(B, S, H, hd).transpose(0, 2, 1, 3)
        k = k.reshape(B, S, H, hd).transpose(0, 2, 1, 3)
        v = v.reshape(B, S, H, hd).transpose(0, 2, 1, 3)
        scores = jnp.einsum('bhqd,bhkd->bhqk', q, k) / jnp.sqrt(jnp.asarray(hd, q.dtype))
        scores = scores + sliding_mask(S)
        attn = jax.nn.softmax(scores, axis=-1)
        ctx = jnp.einsum('bhqk,bhkd->bhqd', attn, v)
        ctx = ctx.transpose(0, 2, 1, 3).reshape(B, S, D)
        return ctx @ w_out.T + b_out

    def _L0_ffn_ref(x, fc1_A, fc1_B, fc2_A, fc2_B, fc1_logits, fc2_logits):
        import jax, jax.numpy as jnp
        import numpy as np
        TOP_K = 32
        TEMPERATURE = 1.0
        PARAM_SCALE = 0.02

        def _compose_weight(logits, A, B):
            vals, idx = jax.lax.top_k(logits, TOP_K)
            w = jax.nn.softmax(vals / TEMPERATURE)
            A_sel = A[idx]
            B_sel = B[idx]
            return jnp.einsum('k,kir,kro->io', w, A_sel, B_sel)
        W1 = _compose_weight(fc1_logits, fc1_A, fc1_B)
        W2 = _compose_weight(fc2_logits, fc2_A, fc2_B)
        h = jax.nn.gelu(jnp.einsum('bsd,df->bsf', x, W1))
        return jnp.einsum('bsf,fd->bsd', h, W2)
    x = L0_attn_input_embeddings
    x = _layernorm(x + _L0_attn_ref(x, L0_attn_token_ids, L0_attn_w_qkv, L0_attn_b_qkv, L0_attn_w_out, L0_attn_b_out), axis=-1)
    x = _layernorm(x + _L0_ffn_ref(x, L0_ffn_fc1_A, L0_ffn_fc1_B, L0_ffn_fc2_A, L0_ffn_fc2_B, L0_ffn_fc1_logits, L0_ffn_fc2_logits), axis=-1)
    return x

_drawn_inputs = setup_inputs


def setup_inputs(seed=0):
    import zlib

    import numpy as np

    out = dict(_drawn_inputs(seed))
    spreads = {'L0_attn_b_qkv': (0.0, 0.1), 'L0_attn_b_out': (0.0, 0.1)}
    factors = {'L0_ffn_fc1_A': 8.0,
     'L0_ffn_fc1_B': 8.0,
     'L0_ffn_fc2_A': 8.0,
     'L0_ffn_fc2_B': 8.0,
     'L0_ffn_fc1_logits': 8.0,
     'L0_ffn_fc2_logits': 8.0}
    for name, (base, spread) in spreads.items():
        noise = np.random.default_rng([zlib.crc32(name.encode()), seed]).standard_normal(out[name].shape)
        drawn = base * np.exp(spread * noise) if base else spread * noise
        out[name] = jnp.asarray(drawn.astype(out[name].dtype))
    for name, factor in factors.items():
        out[name] = (out[name] * factor).astype(out[name].dtype)
    return out
```

```python
from contextlib import ExitStack

import concourse.bass as bass
from concourse import mybir

F32 = mybir.dt.float32
BF16 = mybir.dt.bfloat16
ALU = mybir.AluOpType
ACT = mybir.ActivationFunctionType
AX = mybir.AxisListType

P = 128
B, S, D = 8, 256, 128
H, HD = 16, 8
WIN = 16
HALO = WIN // 2
QB = 32
KW = QB + WIN
NQ = 4
BLOCKS = S // QB
HALF = BLOCKS // 2
NWIN = BLOCKS + 1
XW = NWIN * QB
TILES = S // P
F = 512
FI = F // P
NP, R = 32, 64
CH = NP * R // P
KK = P // R
GT = 4
GROUPS = B * TILES // GT
EPS = 1e-5
SCALE = float(HD) ** -0.5


def block_kernel(nc, x, xt, w_qk_t, w_v_t, b_qkv, w_out_t, b_out, a1_t, b1, a2_t, b2, lg1, lg2, eye, band, qmask, out):
    x_v = x.rearrange("b (t p) d -> p (b t) d", p=P)
    out_v = out.rearrange("b (t p) d -> p (b t) d", p=P)
    a1_v = a1_t.rearrange("(c p) d -> p c d", p=P)
    b1_v = b1.rearrange("(c p) f -> p c f", p=P)
    a2_v = a2_t.rearrange("(c p) f -> p c f", p=P)
    b2_v = b2.rearrange("(c p) o -> p c o", p=P)

    with ExitStack() as ctx:
        def sb(name, shape, dt=F32):
            return ctx.enter_context(nc.sbuf_tensor(name, shape, dt))

        def sem(name):
            return ctx.enter_context(nc.semaphore(name))

        ident = sb("ident", [P, P])
        ident_bf = sb("ident_bf", [P, P], BF16)
        band_f = sb("band_f", [P, 3, KW])
        band_bf = sb("band_bf", [P, 3, NQ, KW], BF16)
        qm = sb("qm", [P, NQ])
        wqkT = sb("wqkT", [P, 2, D])
        wvT = sb("wvT", [P, NQ, NQ * HD])
        woutT = sb("woutT", [P, D])
        bqkv = sb("bqkv", [P, 3])
        bqm = sb("bqm", [P, NQ])
        bout = sb("bout", [P, D])
        row_bias = sb("row_bias", [P, D])
        xT = sb("xT", [P, XW])
        qx = sb("qx", [P, BLOCKS, NQ, QB])
        kx = sb("kx", [P, NQ, S + WIN])
        vx = sb("vx", [P, NWIN, NQ, NQ, HD + 1])
        top = sb("top", [P, 2, HALF * NQ])
        pr = sb("pr", [P, 2, HALF * NQ, 2 * QB])
        pT = sb("pT", [P, 2, HALF, NQ, 2, QB])
        rden = sb("rden", [P, BLOCKS * NQ])
        cx = sb("cx", [P, BLOCKS, NQ * HD])
        cT = sb("cT", [P, BLOCKS, QB])
        z = sb("z", [P, TILES, D])
        stats = sb("stats", [P, TILES, 6])
        mv = sb("mv", [P, TILES, 2])
        rstd = sb("rstd", [P, TILES])
        x1 = sb("x1", [P, TILES, D])
        xr = sb("xr", [P, B * TILES, D])
        x1_all = sb("x1_all", [P, B * TILES, D])
        x1T = sb("x1T", [P, B * S])
        lg = sb("lg", [P, 2, NP])
        lmax = sb("lmax", [P, 2])
        lsh = sb("lsh", [P, 2, NP])
        lexp = sb("lexp", [P, 2, NP])
        lsum = sb("lsum", [P, 2])
        linv = sb("linv", [P, 2])
        wcol = sb("wcol", [P, 2, CH])
        a1s = sb("a1s", [P, CH, D])
        a1w = sb("a1w", [P, CH, D])
        b1s = sb("b1s", [P, CH, F])
        a2s = sb("a2s", [P, CH, F])
        b2s = sb("b2s", [P, CH, D])
        b2w = sb("b2w", [P, CH, D])
        w1 = sb("w1", [P, FI, P])
        w2 = sb("w2", [P, FI, D])
        hT = sb("hT", [P, FI, GT * P])
        zz = sb("zz", [P, GT, D])
        stats2 = sb("stats2", [P, GT, 6])
        mv2 = sb("mv2", [P, GT, 2])
        rstd2 = sb("rstd2", [P, GT])
        yo = sb("yo", [P, GT, D])
        warm = sb("warm", [P, 1])
        epsc = sb("epsc", [P, GT])
        halfc = sb("halfc", [P, GT])
        ps = ctx.enter_context(nc.psum_tensor("ps", [P, 8, 512], F32))

        def scores_ps(u):
            return ps[:, 2 * u:2 * u + 2, 0:2 * NQ * KW]
        qk_ps = ps[:, 4, :]
        x1T_ps = ps[:, 5, 0:S]
        v_ps = ps[:, 6, 0:NWIN * NQ * HD]
        cx_ps = ps[:, 7, 0:BLOCKS * NQ * (HD + 1)]
        y_ps = ps[:, 5, S:S + TILES * D]
        w1_ps = ps[:, 4, :]
        w2_ps = [ps[:, i, 0:D] for i in range(FI)]
        h_ps = [ps[:, 0, :], ps[:, 1, :], ps[:, 2, :], ps[:, 3, :]]
        ff_ps = ps[:, 6, :]

        x_loaded = sem("x_loaded")
        wqk_loaded = sem("wqk_loaded")
        wv_loaded = sem("wv_loaded")
        wout_loaded = sem("wout_loaded")
        resid_loaded = sem("resid_loaded")
        ident_loaded = sem("ident_loaded")
        band_loaded = sem("band_loaded")
        biases_loaded = sem("biases_loaded")
        logits_loaded = sem("logits_loaded")
        bout_loaded = sem("bout_loaded")
        parts_loaded = [sem(f"parts_loaded{n}") for n in range(4)]
        stored = sem("stored")

        xT_cleared = sem("xT_cleared")
        cleared = sem("cleared")
        vx_cleared = sem("vx_cleared")
        consts_made = sem("consts_made")
        warmed = sem("warmed")
        bqm_made = sem("bqm_made")
        rowb_ready = sem("rowb_ready")
        rowb_made = sem("rowb_made")
        lg_step = sem("lg_step")
        lg_exp = sem("lg_exp")
        wcol_made = sem("wcol_made")

        x_biased = sem("x_biased")
        qk_ready = sem("qk_ready")
        qk_placed = sem("qk_placed")
        v_ready = sem("v_ready")
        v_placed = sem("v_placed")
        scored = sem("scored")
        max_found = sem("max_found")
        shifted = sem("shifted")
        exp_done = sem("exp_done")
        p_turned = sem("p_turned")
        attended = sem("attended")
        den_inverted = sem("den_inverted")
        normalised = sem("normalised")
        cx_turned = sem("cx_turned")
        y_ready = sem("y_ready")
        z_added = sem("z_added")
        stats_made = sem("stats_made")
        mv_made = sem("mv_made")
        rstd_made = sem("rstd_made")
        x1_made = sem("x1_made")
        x1_kept = sem("x1_kept")
        x1_turned = sem("x1_turned")
        x1T_copied = sem("x1T_copied")

        a1_scaled = sem("a1_scaled")
        b2_scaled = sem("b2_scaled")
        w1_ready = sem("w1_ready")
        w2_ready = sem("w2_ready")
        w1_copied = sem("w1_copied")
        w2_copied = sem("w2_copied")
        h_ready = sem("h_ready")
        h_done = sem("h_done")
        ff_ready = sem("ff_ready")
        zz_made = sem("zz_made")
        stats2_made = sem("stats2_made")
        mv2_made = sem("mv2_made")
        rstd2_made = sem("rstd2_made")
        yo_made = sem("yo_made")

        block = ctx.enter_context(nc.Block())

        def over_batches(eng, batch):
            batch(0, first=True)
            batch(1)
            with eng.Fori(2, B - 1) as b:
                batch(b)
            batch(B - 1, last=True)

        @block.sync
        def _(sp):
            sp.dma_start(wqkT[:, :, :], w_qk_t.rearrange("d (n m) -> d n m", n=2)).then_inc(wqk_loaded, 16)
            sp.wait_ge(xT_cleared, 1)
            sp.dma_start(xT[:, HALO:HALO + S], xt[:, 0, :]).then_inc(x_loaded, 16)
            sp.dma_start(wvT[:, :, :], w_v_t.rearrange("d (u e) -> d u e", u=NQ)).then_inc(wv_loaded, 16)
            sp.dma_start(band_f[:, :, :], band).then_inc(band_loaded, 16)
            sp.dma_start(woutT[:, :], w_out_t).then_inc(wout_loaded, 16)
            sp.dma_start(xr[:, :, :], x_v).then_inc(resid_loaded, 16)

            def batch(b, first=False, last=False):
                if not last:
                    sp.wait_ge(v_ready, b + 1)
                    sp.dma_start(xT[:, HALO:HALO + S], xt[:, bass.ds(b + 1, 1), :].rearrange("d a s -> d (a s)"))\
                      .then_inc(x_loaded, 16)
                cs = bass.ds(b * (CH // B), CH // B)
                if not first:
                    for n in range(4):
                        sp.wait_ge(parts_loaded[n], 16 * b)
                sp.dma_start(a1s[:, cs, :], a1_v[:, cs, :]).then_inc(parts_loaded[0], 16)
                sp.dma_start(b1s[:, cs, :], b1_v[:, cs, :]).then_inc(parts_loaded[1], 16)
                sp.dma_start(a2s[:, cs, :], a2_v[:, cs, :]).then_inc(parts_loaded[2], 16)
                sp.dma_start(b2s[:, cs, :], b2_v[:, cs, :]).then_inc(parts_loaded[3], 16)

            over_batches(sp, batch)

            with sp.Fori(0, GROUPS) as g:
                sp.wait_ge(yo_made, GT * (g + 1))
                sp.dma_start(out_v[:, bass.ds(g * GT, GT), :], yo[:, :, :]).then_inc(stored, 16)
            sp.wait_ge(stored, 16 * GROUPS)

        @block.tensor
        def _(pe):
            def project(b):
                pe.wait_ge(x_loaded, 16 * (b + 1))
                for n in range(2):
                    mm = pe.matmul(qk_ps[:, n * S:(n + 1) * S], wqkT[:, n, :], xT[:, HALO:HALO + S],
                                   start=True, stop=True)
                mm.then_inc(qk_ready, 1)

            def values(b):
                if not (isinstance(b, int) and b == 0):
                    pe.wait_ge(v_placed, NQ * b)
                for m in range(NWIN):
                    for u in range(NQ):
                        mm = pe.matmul(v_ps[QB * u:QB * (u + 1), m * NQ * HD:(m + 1) * NQ * HD],
                                       xT[:, m * QB:(m + 1) * QB], wvT[:, u, :], start=True, stop=True)
                mm.then_inc(v_ready, 1)

            def scores(b):
                pe.wait_ge(qk_placed, 8 * (b + 1))
                for u in range(2):
                    for n in range(HALF):
                        m = u * HALF + n
                        o = scores_ps(u)[:, n // 2, (n % 2) * NQ * KW:(n % 2 + 1) * NQ * KW]
                        kind = 0 if m == 0 else 2 if m == BLOCKS - 1 else 1
                        pe.matmul(o, qx[:, m, :, :], kx[:, :, m * QB:m * QB + KW],
                                  start=True, stop=False)
                        mm = pe.matmul(o, ident_bf[:, :], band_bf[:, kind, :, :], start=False, stop=True)
                        if n % 2 == 1:
                            mm.then_inc(scored, 1)

            def attend(b):
                pe.wait_ge(v_placed, 4 * (b + 1))
                for u in range(2):
                    for n in range(HALF):
                        if n == 0:
                            pe.wait_ge(p_turned, 3 * b + u + 1)
                        if u == 1 and n == 2:
                            pe.wait_ge(p_turned, 3 * b + 3)
                        m = u * HALF + n
                        for j in range(NQ):
                            o = cx_ps[QB * j:QB * (j + 1), m * NQ * (HD + 1):(m + 1) * NQ * (HD + 1)]
                            for w in range(2):
                                mm = pe.matmul(o, pT[:, u, n, j, w, :], vx[:, m + w, j, :, :],
                                               start=(w == 0), stop=(w == 1))
                mm.then_inc(attended, 1)

            def project_out(b):
                if not (isinstance(b, int) and b == 0):
                    pe.wait_ge(x1T_copied, b)
                pe.wait_ge(cx_turned, b + 1)
                for t in range(TILES):
                    mm = pe.matmul(y_ps[:, t * D:(t + 1) * D], cT[:, t * HALF:(t + 1) * HALF, :],
                                   woutT[:, :], start=True, stop=True)
                mm.then_inc(y_ready, 1)

            def turn_x1(b):
                pe.wait_ge(x1_made, 2 * b + 2)
                for t in range(TILES):
                    mm = pe.transpose(x1T_ps[:, t * P:(t + 1) * P], x1[:, t, :], ident[:, :])
                mm.then_inc(x1_turned, 1)

            pe.wait_ge(wqk_loaded, 16)
            project(0)
            pe.wait_ge(wv_loaded, 16)
            values(0)
            pe.wait_ge(biases_loaded, 32)
            pe.wait_ge(wout_loaded, 16)
            pe.matmul(ps[:, 0, 0:D], bqkv[:, 2:3].broadcast_to([P, P]), woutT[:, :],
                      start=True, stop=True).then_inc(rowb_ready, 1)
            pe.wait_ge(ident_loaded, 16)
            pe.wait_ge(consts_made, 2)
            pe.wait_ge(cleared, 3)
            pe.wait_ge(rowb_made, 1)

            def batch(b, first=False, last=False):
                scores(b)
                if not (isinstance(b, int) and b < 2):
                    turn_x1(b - 2)
                if not last:
                    project(b + 1)
                if not first:
                    project_out(b - 1)
                if not last:
                    values(b + 1)
                attend(b)

            over_batches(pe, batch)

            turn_x1(B - 2)
            for n in range(2):
                pe.wait_ge(parts_loaded[n], 16 * B)
            pe.wait_ge(a1_scaled, B)
            for c in range(CH):
                mm = pe.matmul(w1_ps, a1w[:, c, :], b1s[:, c, :], start=(c == 0), stop=(c == CH - 1))
            mm.then_inc(w1_ready, 1)
            project_out(B - 1)
            pe.wait_ge(parts_loaded[2], 16 * B)
            pe.wait_ge(b2_scaled, B)
            for i in range(FI):
                for c in range(CH):
                    mm = pe.matmul(w2_ps[i], a2s[:, c, i * P:(i + 1) * P], b2w[:, c, :],
                                   start=(c == 0), stop=(c == CH - 1))
                mm.then_inc(w2_ready, 1)
                if i == FI // 2 - 1:
                    turn_x1(B - 1)

            pe.wait_ge(w1_copied, 1)

            def ff_out(g, i):
                pe.wait_ge(h_done, FI * g + i + 1)
                for t in range(GT):
                    mm = pe.matmul(ff_ps[:, t * D:(t + 1) * D], hT[:, i, t * P:(t + 1) * P], w2[:, i, :],
                                   start=(i == 0 and t == 0), stop=(i == FI - 1), skip_group_check=True)
                return mm

            def group(g, first=False):
                for i in range(FI):
                    if first:
                        pe.wait_ge(w2_copied, i + 1)
                    pe.matmul(h_ps[i], w1[:, i, :], x1T[:, bass.ds(g * GT * P, GT * P)],
                              start=True, stop=True).then_inc(h_ready, 1)
                    if i == 1 and first:
                        pe.wait_ge(w2_copied, FI)
                    if i == 1 and not first:
                        pe.wait_ge(zz_made, g)
                    if i >= 1:
                        ff_out(g, i - 1)
                ff_out(g, FI - 1).then_inc(ff_ready, 1)

            group(0, first=True)
            pe.wait_ge(x1T_copied, B)
            with pe.Fori(1, GROUPS) as g:
                group(g)

        @block.scalar
        def _(act):
            act.dma_start(bqkv[:, :], b_qkv).then_inc(biases_loaded, 16)
            act.dma_start(qm[:, :], qmask).then_inc(biases_loaded, 16)
            act.wait_ge(xT_cleared, 1)
            act.activation(warm[:, :], xT[:, 0:1], ACT.Exp).then_inc(warmed, 1)
            act.dma_start(ident[:, :], eye).then_inc(ident_loaded, 16)
            act.dma_start(bout[:, :], b_out.rearrange("(a n) -> a n", a=1).broadcast_to([P, D]))\
               .then_inc(bout_loaded, 16)
            act.dma_start(lg[:, 0, :], lg1.rearrange("(a n) -> a n", a=1).broadcast_to([P, NP]))\
               .then_inc(logits_loaded, 16)
            act.dma_start(lg[:, 1, :], lg2.rearrange("(a n) -> a n", a=1).broadcast_to([P, NP]))\
               .then_inc(logits_loaded, 16)

            def place_qk(b):
                act.wait_ge(qk_ready, b + 1)
                for u in range(NQ):
                    act.activation(qx[:, :, u, :], qk_ps[:, 0:S].rearrange("p (m q) -> p m q", q=QB), ACT.Identity, bias=bqm[:, u:u + 1],
                                   scale=qm[:, u:u + 1]).then_inc(qk_placed, 1)
                for j in range(NQ):
                    r = slice(QB * j, QB * (j + 1))
                    act.activation(kx[r, j, HALO:HALO + S], qk_ps[r, S:2 * S], ACT.Identity,
                                   bias=bqkv[r, 1:2]).then_inc(qk_placed, 1)

            def place_v(b):
                act.wait_ge(v_ready, b + 1)
                for u in range(NQ):
                    r = slice(QB * u, QB * (u + 1))
                    act.activation(vx[r, :, :, u, 0:HD],
                                   v_ps[r, :].rearrange("p (m j d) -> p m j d", m=NWIN, j=NQ),
                                   ACT.Copy).then_inc(v_placed, 1)

            def exponentials(b, u):
                act.wait_ge(shifted, 2 * b + u + 1)
                act.activation(pr[:, u, :, 0:KW], pr[:, u, :, 0:KW], ACT.Exp).then_inc(exp_done, 1)

            def copy_x1T(b):
                act.wait_ge(x1_turned, b + 1)
                act.activation(x1T[:, bass.ds(b * S, S)], x1T_ps, ACT.Copy).then_inc(x1T_copied, 1)

            act.wait_ge(cleared, 3)
            act.wait_ge(bqm_made, 1)
            place_qk(0)
            act.wait_ge(vx_cleared, 5)
            place_v(0)

            act.wait_ge(lg_step, 2)
            act.activation(lexp[:, :, :], lsh[:, :, :], ACT.Exp).then_inc(lg_exp, 1)

            def batch(b, first=False, last=False):
                exponentials(b, 0)
                if not (isinstance(b, int) and b < 2):
                    copy_x1T(b - 2)
                exponentials(b, 1)
                if not last:
                    place_qk(b + 1)
                    act.wait_ge(attended, b + 1)
                    place_v(b + 1)

            over_batches(act, batch)
            copy_x1T(B - 2)
            for i in range(FI):
                act.wait_ge(w2_ready, i + 1)
                act.activation(w2[:, i, :], w2_ps[i], ACT.Copy).then_inc(w2_copied, 1)
                if i == FI // 2 - 1:
                    copy_x1T(B - 1)

            def gelu(g, first=False):
                for i in range(FI):
                    act.wait_ge(h_ready, FI * g + i + 1)
                    if i == 0 and not first:
                        act.wait_ge(ff_ready, g)
                    act.activation(hT[:, i, :], h_ps[i], ACT.Gelu_apprx_tanh).then_inc(h_done, 1)

            gelu(0, first=True)
            with act.Fori(1, GROUPS) as g:
                gelu(g)

        @block.vector
        def _(dve):
            dve.memset(xT[:, :], 0.0).then_inc(xT_cleared, 1)
            dve.memset(kx[:, :, :], 0.0).then_inc(cleared, 1)
            dve.memset(pr[:, 0, :, KW:], 0.0).then_inc(cleared, 1)
            dve.memset(pr[:, 1, :, KW:], 0.0).then_inc(cleared, 1)
            dve.wait_ge(vx_cleared, 1)
            for u in range(NQ):
                dve.memset(vx[QB * u:QB * (u + 1), :, :, u, HD], 1.0).then_inc(vx_cleared, 1)
            dve.wait_ge(biases_loaded, 32)
            dve.tensor_scalar(bqm[:, :], qm[:, :], bqkv[:, 0:1], None, ALU.mult).then_inc(bqm_made, 1)
            dve.wait_ge(band_loaded, 16)
            dve.tensor_copy(band_bf[:, :, :, :], band_f[:, :, :].unsqueeze(2).broadcast_to([P, 3, NQ, KW]))\
               .then_inc(consts_made, 1)
            dve.wait_ge(ident_loaded, 16)
            dve.tensor_copy(ident_bf[:, :], ident[:, :]).then_inc(consts_made, 1)
            dve.wait_ge(bout_loaded, 16)
            dve.wait_ge(rowb_ready, 1)
            dve.tensor_tensor(row_bias[:, :], ps[:, 0, 0:D], bout[:, :], ALU.add).then_inc(rowb_made, 1)

            def shift(b, u):
                s4 = scores_ps(u).rearrange("p c (g k) -> p c g k", k=KW)
                t3 = top[:, u, :].rearrange("p (c g) -> p c g", c=2)
                for c in range(2):
                    dve.wait_ge(scored, 4 * b + 2 * u + c + 1)
                    dve.tensor_reduce(t3[:, c, :], s4[:, c, :, :], AX.X, ALU.max).then_inc(max_found, 1)
                dve.wait_ge(max_found, 4 * b + 2 * u + 2)
                dve.tensor_tensor(pr[:, u, :, 0:KW].rearrange("p (c g) k -> p c g k", c=2), s4,
                                  t3.unsqueeze(3).broadcast_to([P, 2, HALF * NQ // 2, KW]),
                                  ALU.subtract).then_inc(shifted, 1)

            def add_residual(b):
                dve.wait_ge(y_ready, b + 1)
                dve.wait_ge(x_biased, b + 1)
                if not (isinstance(b, int) and b == 0):
                    dve.wait_ge(x1_made, 2 * b)
                dve.tensor_tensor(z[:, :, :], y_ps.rearrange("p (t d) -> p t d", t=TILES),
                                  xr[:, bass.ds(b * TILES, TILES), :], ALU.add).then_inc(z_added, 1)
                dve.wait_ge(z_added, b + 1)
                for t in range(TILES):
                    dve.bn_stats(stats[:, t, :], z[:, t, :]).then_inc(stats_made, 1)

            def moments(b):
                for t in range(TILES):
                    dve.bn_aggr(mv[:, t, :], stats[:, t, :]).then_inc(mv_made, 1)

            def turn_p(b, u, blocks=slice(0, HALF)):
                g = slice(blocks.start * NQ, blocks.stop * NQ)
                dve.wait_ge(exp_done, 2 * b + u + 1)
                dve.transpose(pT[:, u, blocks, :, :, :].rearrange("p n j w q -> p (n j w q)"),
                              pr[:, u, g, :].rearrange("p g k -> p (g k)")).then_inc(p_turned, 1)

            def normalise(b):
                c3 = cx_ps.rearrange("p (g e) -> p g e", e=HD + 1)
                dve.wait_ge(attended, b + 1)
                dve.reciprocal(rden[:, :], c3[:, :, HD]).then_inc(den_inverted, 1)
                dve.wait_ge(den_inverted, b + 1)
                dve.tensor_tensor(cx[:, :, :].rearrange("p m (u d) -> p (m u) d", u=NQ), c3[:, :, 0:HD],
                                  rden[:, :].unsqueeze(2).broadcast_to([P, BLOCKS * NQ, HD]),
                                  ALU.mult).then_inc(normalised, 1)
                dve.wait_ge(normalised, b + 1)
                dve.transpose(cT[:, :, :].rearrange("p m q -> p (m q)"),
                              cx[:, :, :].rearrange("p m e -> p (m e)")).then_inc(cx_turned, 1)

            def batch(b, first=False, last=False):
                shift(b, 0)
                shift(b, 1)
                turn_p(b, 0)
                turn_p(b, 1, slice(0, HALF // 2))
                if not first:
                    add_residual(b - 1)
                    dve.wait_ge(stats_made, TILES * b)
                turn_p(b, 1, slice(HALF // 2, HALF))
                if not first:
                    moments(b - 1)
                normalise(b)

            dve.wait_ge(logits_loaded, 32)
            dve.tensor_reduce(lmax[:, :], lg[:, :, :], AX.X, ALU.max).then_inc(lg_step, 1)
            dve.wait_ge(lg_step, 1)
            dve.tensor_tensor(lsh[:, :, :], lg[:, :, :], lmax[:, :].unsqueeze(2).broadcast_to([P, 2, NP]),
                              ALU.subtract).then_inc(lg_step, 1)
            dve.wait_ge(lg_exp, 1)
            dve.tensor_reduce(lsum[:, :], lexp[:, :, :], AX.X, ALU.add).then_inc(lg_step, 1)
            dve.wait_ge(lg_step, 3)
            dve.reciprocal(linv[:, :], lsum[:, :]).then_inc(lg_step, 1)
            dve.wait_ge(lg_step, 4)
            for k in range(KK):
                r = slice(R * k, R * (k + 1))
                for n in range(2):
                    dve.tensor_scalar(wcol[r, n, :], lexp[r, n, k::KK], linv[r, n:n + 1], None,
                                      ALU.mult).then_inc(wcol_made, 1)

            over_batches(dve, batch)
            dve.wait_ge(w1_ready, 1)
            dve.tensor_copy(w1[:, :, :], w1_ps.rearrange("p (i q) -> p i q", i=FI)).then_inc(w1_copied, 1)
            add_residual(B - 1)
            dve.wait_ge(stats_made, TILES * B)
            moments(B - 1)

            def finish(g, first=False):
                dve.wait_ge(ff_ready, g + 1)
                if first:
                    dve.wait_ge(x1_kept, B)
                else:
                    dve.wait_ge(yo_made, GT * g)
                dve.tensor_tensor(zz[:, :, :], ff_ps.rearrange("p (t d) -> p t d", t=GT),
                                  x1_all[:, bass.ds(g * GT, GT), :], ALU.add).then_inc(zz_made, 1)
                dve.wait_ge(zz_made, g + 1)
                for t in range(GT):
                    dve.bn_stats(stats2[:, t, :], zz[:, t, :]).then_inc(stats2_made, 1)
                dve.wait_ge(stats2_made, GT * (g + 1))
                for t in range(GT):
                    dve.bn_aggr(mv2[:, t, :], stats2[:, t, :]).then_inc(mv2_made, 1)
                if not first:
                    dve.wait_ge(stored, 16 * g)
                dve.wait_ge(rstd2_made, 2 * g + 2)
                for t in range(GT):
                    dve.tensor_scalar(yo[:, t, :], zz[:, t, :], mv2[:, t, 0:1], rstd2[:, t:t + 1],
                                      ALU.subtract, ALU.mult).then_inc(yo_made, 1)

            for g in range(GROUPS):
                finish(g, first=(g == 0))

        @block.gpsimd
        def _(pool):
            pool.memset(vx[:, :, :, :, :], 0.0).then_inc(vx_cleared, 1)
            pool.memset(epsc[:, :], EPS).then_inc(rstd_made, 1)
            pool.memset(halfc[:, :], -0.5).then_inc(rstd_made, 1)
            pool.wait_ge(rowb_made, 1)
            pool.wait_ge(resid_loaded, 16)

            def bias_x(b):
                xb = xr[:, bass.ds(b * TILES, TILES), :]
                pool.tensor_tensor(xb, xb,
                                   row_bias[:, :].unsqueeze(1).broadcast_to([P, TILES, D]),
                                   ALU.add).then_inc(x_biased, 1)

            def scale_parts(b):
                cs = bass.ds(b * (CH // B), CH // B)
                pool.wait_ge(parts_loaded[0], 16 * (b + 1))
                pool.wait_ge(parts_loaded[3], 16 * (b + 1))
                pool.tensor_tensor(a1w[:, cs, :], a1s[:, cs, :],
                                   wcol[:, 0, cs].unsqueeze(2).broadcast_to([P, CH // B, D]),
                                   ALU.mult).then_inc(a1_scaled, 1)
                pool.tensor_tensor(b2w[:, cs, :], b2s[:, cs, :],
                                   wcol[:, 1, cs].unsqueeze(2).broadcast_to([P, CH // B, D]),
                                   ALU.mult).then_inc(b2_scaled, 1)

            def normalise_z(b, first=False):
                pool.wait_ge(mv_made, TILES * (b + 1))
                pool.tensor_tensor(rstd[:, :], mv[:, :, 1], epsc[:, 0:TILES], ALU.add).then_inc(rstd_made, 1)
                pool.wait_ge(rstd_made, 2 * b + 3)
                pool.tensor_tensor(rstd[:, :], rstd[:, :], halfc[:, 0:TILES], ALU.pow).then_inc(rstd_made, 1)
                pool.wait_ge(rstd_made, 2 * b + 4)
                if not first:
                    pool.wait_ge(x1_turned, b)
                    pool.wait_ge(x1_kept, b)
                pool.tensor_tensor(x1[:, :, :], z[:, :, :], mv[:, :, 0:1].broadcast_to([P, TILES, D]),
                                   ALU.subtract).then_inc(x1_made, 1)
                pool.wait_ge(x1_made, 2 * b + 1)
                pool.tensor_tensor(x1[:, :, :], x1[:, :, :], rstd[:, :].unsqueeze(2).broadcast_to([P, TILES, D]),
                                   ALU.mult).then_inc(x1_made, 1)
                pool.wait_ge(x1_made, 2 * b + 2)
                pool.tensor_copy(x1_all[:, bass.ds(b * TILES, TILES), :], x1[:, :, :]).then_inc(x1_kept, 1)

            bias_x(0)
            bias_x(1)
            pool.wait_ge(wcol_made, 4)
            scale_parts(0)
            normalise_z(0, first=True)
            with pool.Fori(1, B - 1) as b:
                bias_x(b + 1)
                scale_parts(b)
                normalise_z(b)
            scale_parts(B - 1)
            normalise_z(B - 1)

            with pool.Fori(0, GROUPS) as g:
                pool.wait_ge(mv2_made, GT * (g + 1))
                pool.tensor_tensor(rstd2[:, :], mv2[:, :, 1], epsc[:, :], ALU.add).then_inc(rstd2_made, 1)
                pool.wait_ge(rstd2_made, 2 * g + 1)
                pool.tensor_tensor(rstd2[:, :], rstd2[:, :], halfc[:, :], ALU.pow).then_inc(rstd2_made, 1)


def shape_constants():
    import numpy as np

    eye = np.eye(P, dtype=np.float32)
    r = np.arange(P)[:, None] % QB
    w = np.arange(KW)[None, :]
    band = np.stack([(w >= r) & (w <= r + WIN) & (w >= HALO),
                     (w >= r) & (w <= r + WIN),
                     (w >= r) & (w <= r + WIN) & (w < KW - HALO)], axis=1)
    band = np.where(band, 0.0, -1e30).astype(np.float32)
    qmask = ((np.arange(P)[:, None] // HD) % NQ == np.arange(NQ)[None, :]) * SCALE
    return eye, band, qmask.astype(np.float32)


def kernel(**inputs):
    import numpy as np
    import concourse.bacc as bacc
    from concourse.bass_utils import run_bass_kernel_spmd

    eye, band, qmask = shape_constants()
    x = np.asarray(inputs["L0_attn_input_embeddings"])
    w_qkv = np.asarray(inputs["L0_attn_w_qkv"])
    rows = {
        "x": x,
        "x_t": x.transpose(2, 0, 1),
        "w_qk_t": w_qkv[:2 * D].T,
        "w_v_t": w_qkv[2 * D:].T.reshape(D, NQ, NQ, HD).transpose(0, 2, 1, 3).reshape(D, D),
        "b_qkv": np.asarray(inputs["L0_attn_b_qkv"]).reshape(3, D).T,
        "w_out_t": np.asarray(inputs["L0_attn_w_out"]).T,
        "b_out": np.asarray(inputs["L0_attn_b_out"]),
        "fc1_a_t": np.asarray(inputs["L0_ffn_fc1_A"]).transpose(0, 2, 1).reshape(NP * R, D),
        "fc1_b": np.asarray(inputs["L0_ffn_fc1_B"]).reshape(NP * R, F),
        "fc2_a_t": np.asarray(inputs["L0_ffn_fc2_A"]).transpose(0, 2, 1).reshape(NP * R, F),
        "fc2_b": np.asarray(inputs["L0_ffn_fc2_B"]).reshape(NP * R, D),
        "fc1_logits": np.asarray(inputs["L0_ffn_fc1_logits"]),
        "fc2_logits": np.asarray(inputs["L0_ffn_fc2_logits"]),
    }
    arrays = {"in_" + n: np.ascontiguousarray(a) for n, a in rows.items()}
    arrays.update(c_eye=eye, c_band=band, c_qmask=qmask)
    nc = bacc.Bacc("TRN2", target_bir_lowering=False, num_devices=1)
    args = [nc.dram_tensor(n, a.shape, F32, kind="ExternalInput").ap() for n, a in arrays.items()]
    out = nc.dram_tensor("out", (B, S, D), F32, kind="ExternalOutput").ap()
    block_kernel(nc, *args, out)
    r = run_bass_kernel_spmd(nc, [arrays], core_ids=[0])
    return r.results[0]["out"]
```

```python
from contextlib import ExitStack

import concourse.bass as bass
from concourse import mybir

F32 = mybir.dt.float32
BF16 = mybir.dt.bfloat16
ALU = mybir.AluOpType
ACT = mybir.ActivationFunctionType
AX = mybir.AxisListType

P = 128
B, S, D = 8, 256, 128
H, HD = 16, 8
WIN = 16
HALO = WIN // 2
QB = 32
KW = QB + WIN
NQ = 4
BLOCKS = S // QB
HALF = BLOCKS // 2
NWIN = BLOCKS + 1
XW = NWIN * QB
TILES = S // P
F = 512
FI = F // P
NP, R = 32, 64
CH = NP * R // P
CB = 2 * CH // B
MID = CH // CB
KK = P // R
GT = 4
GROUPS = B * TILES // GT
EPS = 1e-5
SCALE = float(HD) ** -0.5


def block_kernel(nc, x, xt, w_qk_t, w_v_t, b_qkv, w_out_t, b_out, narrow, wide, lg1, lg2, eye, band, qmask, out):
    x_v = x.rearrange("b (t p) d -> p (b t) d", p=P)
    out_v = out.rearrange("b (t p) d -> p (b t) d", p=P)
    narrow_v = narrow.rearrange("(c p) d -> p c d", p=P)
    wide_v = wide.rearrange("(c p) f -> p c f", p=P)

    with ExitStack() as ctx:
        def sb(name, shape, dt=F32):
            return ctx.enter_context(nc.sbuf_tensor(name, shape, dt))

        def sem(name):
            return ctx.enter_context(nc.semaphore(name))

        ident = sb("ident", [P, P])
        ident_bf = sb("ident_bf", [P, P], BF16)
        band_f = sb("band_f", [P, 3, KW])
        band_bf = sb("band_bf", [P, 3, NQ, KW], BF16)
        qm = sb("qm", [P, NQ])
        wqkT = sb("wqkT", [P, 2, D])
        wvT = sb("wvT", [P, NQ, NQ * HD])
        woutT = sb("woutT", [P, D])
        bqkv = sb("bqkv", [P, 3])
        bqm = sb("bqm", [P, NQ])
        bout = sb("bout", [P, D])
        row_bias = sb("row_bias", [P, D])
        xT = sb("xT", [P, XW])
        qx = sb("qx", [P, BLOCKS, NQ, QB])
        kx = sb("kx", [P, NQ, S + WIN])
        vx = sb("vx", [P, NWIN, NQ, NQ, HD + 1])
        top = sb("top", [P, 2, HALF * NQ])
        pr = sb("pr", [P, 2, HALF * NQ, 2 * QB])
        pT = sb("pT", [P, 2, HALF, NQ, 2, QB])
        rden = sb("rden", [P, BLOCKS * NQ])
        cx = sb("cx", [P, BLOCKS, NQ * HD])
        cT = sb("cT", [P, BLOCKS, QB])
        z = sb("z", [P, TILES, D])
        stats = sb("stats", [P, TILES, 6])
        mv = sb("mv", [P, TILES, 2])
        rstd = sb("rstd", [P, TILES])
        x1 = sb("x1", [P, TILES, D])
        xr = sb("xr", [P, B * TILES, D])
        x1_all = sb("x1_all", [P, B * TILES, D])
        x1T = sb("x1T", [P, B * S])
        lg = sb("lg", [P, 2, NP])
        lmax = sb("lmax", [P, 2])
        lsh = sb("lsh", [P, 2, NP])
        lexp = sb("lexp", [P, 2, NP])
        lsum = sb("lsum", [P, 2])
        linv = sb("linv", [P, 2])
        wcol = sb("wcol", [P, 2 * CH])
        nar = sb("nar", [P, 2 * CH, D])
        narw = sb("narw", [P, CB, D])
        wid = sb("wid", [P, 2 * CH, F])
        w1 = sb("w1", [P, FI, P])
        w2t = sb("w2t", [P, F])
        w2 = sb("w2", [P, FI, D])
        hT = sb("hT", [P, FI, GT * P])
        zz = sb("zz", [P, GT, D])
        stats2 = sb("stats2", [P, GT, 6])
        mv2 = sb("mv2", [P, GT, 2])
        rstd2 = sb("rstd2", [P, GT])
        yo = sb("yo", [P, GT, D])
        warm = sb("warm", [P, 1])
        epsc = sb("epsc", [P, GT])
        halfc = sb("halfc", [P, GT])
        ps = ctx.enter_context(nc.psum_tensor("ps", [P, 8, 512], F32))

        def scores_ps(u):
            return ps[:, 2 * u:2 * u + 2, 0:2 * NQ * KW]
        qk_ps = ps[:, 4, :]
        yt_ps = ps[:, 5, 0:S]
        v_ps = ps[:, 6, 0:NWIN * NQ * HD]
        C0 = NWIN * NQ * HD
        cx_ps = ps[:, 5:7, C0:C0 + HALF * NQ * (HD + 1)]
        w_ps = ps[:, 7, :]
        w2_ps = ps[:, 4, :]
        h_ps = [ps[:, 0, :], ps[:, 1, :], ps[:, 2, :], ps[:, 3, :]]
        ff_ps = ps[:, 6, :]

        x_loaded = sem("x_loaded")
        wqk_loaded = sem("wqk_loaded")
        wv_loaded = sem("wv_loaded")
        wout_loaded = sem("wout_loaded")
        resid_loaded = sem("resid_loaded")
        ident_loaded = sem("ident_loaded")
        band_loaded = sem("band_loaded")
        biases_loaded = sem("biases_loaded")
        logits_loaded = sem("logits_loaded")
        bout_loaded = sem("bout_loaded")
        parts_loaded = [sem(f"parts_loaded{n}") for n in range(2)]
        stored = sem("stored")

        xT_cleared = sem("xT_cleared")
        cleared = sem("cleared")
        vx_cleared = sem("vx_cleared")
        consts_made = sem("consts_made")
        warmed = sem("warmed")
        bqm_made = sem("bqm_made")
        rowb_ready = sem("rowb_ready")
        rowb_made = sem("rowb_made")
        lg_step = sem("lg_step")
        lg_exp = sem("lg_exp")
        wcol_made = sem("wcol_made")

        x_biased = sem("x_biased")
        qk_ready = sem("qk_ready")
        qk_placed = sem("qk_placed")
        v_ready = sem("v_ready")
        v_placed = sem("v_placed")
        scored = sem("scored")
        max_found = sem("max_found")
        shifted = sem("shifted")
        exp_done = sem("exp_done")
        p_turned = sem("p_turned")
        attended = sem("attended")
        den_inverted = sem("den_inverted")
        normalised = sem("normalised")
        cx_turned = sem("cx_turned")
        y_ready = sem("y_ready")
        z_added = sem("z_added")
        stats_made = sem("stats_made")
        mv_made = sem("mv_made")
        rstd_made = sem("rstd_made")
        x1_made = sem("x1_made")
        x1_kept = sem("x1_kept")
        x1_turned = sem("x1_turned")
        x1T_copied = sem("x1T_copied")

        narrow_scaled = sem("narrow_scaled")
        composed = sem("composed")
        w1_copied = sem("w1_copied")
        w2t_copied = sem("w2t_copied")
        w2_ready = sem("w2_ready")
        w2_copied = sem("w2_copied")
        h_ready = sem("h_ready")
        h_done = sem("h_done")
        ff_ready = sem("ff_ready")
        zz_made = sem("zz_made")
        stats2_made = sem("stats2_made")
        mv2_made = sem("mv2_made")
        rstd2_made = sem("rstd2_made")
        yo_made = sem("yo_made")

        block = ctx.enter_context(nc.Block())

        def over_batches(eng, batch):
            batch(0, first=True)
            batch(1)
            with eng.Fori(2, MID) as b:
                batch(b)
            batch(MID, mid=True)
            with eng.Fori(MID + 1, B - 1) as b:
                batch(b)
            batch(B - 1, last=True)

        @block.sync
        def _(sp):
            sp.dma_start(wqkT[:, :, :], w_qk_t.rearrange("d (n m) -> d n m", n=2)).then_inc(wqk_loaded, 16)
            sp.wait_ge(xT_cleared, 1)
            sp.dma_start(xT[:, HALO:HALO + S], xt[:, 0, :]).then_inc(x_loaded, 16)
            sp.dma_start(wvT[:, :, :], w_v_t.rearrange("d (u e) -> d u e", u=NQ)).then_inc(wv_loaded, 16)
            sp.dma_start(band_f[:, :, :], band).then_inc(band_loaded, 16)
            sp.dma_start(woutT[:, :], w_out_t).then_inc(wout_loaded, 16)

            def load_parts(b):
                cs = bass.ds(b * CB, CB)
                if not (isinstance(b, int) and b == 0):
                    for n in range(2):
                        sp.wait_ge(parts_loaded[n], 16 * b)
                sp.dma_start(nar[:, cs, :], narrow_v[:, cs, :]).then_inc(parts_loaded[0], 16)
                sp.dma_start(wid[:, cs, :], wide_v[:, cs, :]).then_inc(parts_loaded[1], 16)

            load_parts(0)
            sp.dma_start(xr[:, :, :], x_v).then_inc(resid_loaded, 16)

            def batch(b, first=False, mid=False, last=False):
                if not last:
                    sp.wait_ge(v_ready, b + 1)
                    sp.dma_start(xT[:, HALO:HALO + S], xt[:, bass.ds(b + 1, 1), :].rearrange("d a s -> d (a s)"))\
                      .then_inc(x_loaded, 16)
                    load_parts(b + 1)

            over_batches(sp, batch)

            with sp.Fori(0, GROUPS) as g:
                sp.wait_ge(yo_made, GT * (g + 1))
                sp.dma_start(out_v[:, bass.ds(g * GT, GT), :], yo[:, :, :]).then_inc(stored, 16)
            sp.wait_ge(stored, 16 * GROUPS)

        @block.tensor
        def _(pe):
            def project(b):
                pe.wait_ge(x_loaded, 16 * (b + 1))
                for n in range(2):
                    mm = pe.matmul(qk_ps[:, n * S:(n + 1) * S], wqkT[:, n, :], xT[:, HALO:HALO + S],
                                   start=True, stop=True)
                mm.then_inc(qk_ready, 1)

            def values(b):
                if not (isinstance(b, int) and b == 0):
                    pe.wait_ge(v_placed, NQ * b)
                for m in range(NWIN):
                    for u in range(NQ):
                        mm = pe.matmul(v_ps[QB * u:QB * (u + 1), m * NQ * HD:(m + 1) * NQ * HD],
                                       xT[:, m * QB:(m + 1) * QB], wvT[:, u, :], start=True, stop=True)
                mm.then_inc(v_ready, 1)

            def scores(b):
                pe.wait_ge(qk_placed, 8 * (b + 1))
                for u in range(2):
                    for n in range(HALF):
                        m = u * HALF + n
                        o = scores_ps(u)[:, n // 2, (n % 2) * NQ * KW:(n % 2 + 1) * NQ * KW]
                        kind = 0 if m == 0 else 2 if m == BLOCKS - 1 else 1
                        pe.matmul(o, qx[:, m, :, :], kx[:, :, m * QB:m * QB + KW],
                                  start=True, stop=False)
                        mm = pe.matmul(o, ident_bf[:, :], band_bf[:, kind, :, :], start=False, stop=True)
                        if n % 2 == 1:
                            mm.then_inc(scored, 1)

            def attend(b):
                pe.wait_ge(v_placed, 4 * (b + 1))
                if not (isinstance(b, int) and b == 0):
                    pe.wait_ge(z_added, b)
                for u in range(2):
                    for n in range(HALF):
                        if n == 0:
                            pe.wait_ge(p_turned, 3 * b + u + 1)
                        if u == 1 and n == 2:
                            pe.wait_ge(p_turned, 3 * b + 3)
                        m = u * HALF + n
                        for j in range(NQ):
                            o = cx_ps[QB * j:QB * (j + 1), u, n * NQ * (HD + 1):(n + 1) * NQ * (HD + 1)]
                            for w in range(2):
                                mm = pe.matmul(o, pT[:, u, n, j, w, :], vx[:, m + w, j, :, :],
                                               start=(w == 0), stop=(w == 1))
                mm.then_inc(attended, 1)

            def project_out(b):
                if not (isinstance(b, int) and b == 0):
                    pe.wait_ge(x1T_copied, b)
                pe.wait_ge(cx_turned, b + 1)
                for t in range(TILES):
                    mm = pe.matmul(yt_ps[:, t * D:(t + 1) * D], cT[:, t * HALF:(t + 1) * HALF, :],
                                   woutT[:, :], start=True, stop=True)
                mm.then_inc(y_ready, 1)

            def turn_x1(b):
                if not (isinstance(b, int) and b == B - 1):
                    pe.wait_ge(normalised, b + 2)
                pe.wait_ge(x1_made, 2 * b + 2)
                for t in range(TILES):
                    mm = pe.transpose(yt_ps[:, t * P:(t + 1) * P], x1[:, t, :], ident[:, :])
                mm.then_inc(x1_turned, 1)

            def compose(b, start=False, stop=False):
                pe.wait_ge(parts_loaded[1], 16 * (b + 1))
                pe.wait_ge(narrow_scaled, b + 1)
                for c in range(CB):
                    mm = pe.matmul(w_ps, narw[:, c, :],
                                   wid[:, bass.ds(b * CB + c, 1), :].rearrange("p a f -> p (a f)"),
                                   start=(start and c == 0), stop=(stop and c == CB - 1), skip_group_check=True)
                mm.then_inc(composed, 1)

            pe.wait_ge(wqk_loaded, 16)
            project(0)
            pe.wait_ge(wv_loaded, 16)
            values(0)
            pe.wait_ge(biases_loaded, 32)
            pe.wait_ge(wout_loaded, 16)
            pe.matmul(ps[:, 0, 0:D], bqkv[:, 2:3].broadcast_to([P, P]), woutT[:, :],
                      start=True, stop=True).then_inc(rowb_ready, 1)
            pe.wait_ge(ident_loaded, 16)
            pe.wait_ge(consts_made, 2)
            pe.wait_ge(cleared, 3)
            pe.wait_ge(rowb_made, 1)

            def batch(b, first=False, mid=False, last=False):
                scores(b)
                if not (isinstance(b, int) and b < 2):
                    turn_x1(b - 2)
                if not last:
                    project(b + 1)
                if mid:
                    pe.wait_ge(w1_copied, 1)
                compose(b, start=(first or mid), stop=last)
                if not first:
                    project_out(b - 1)
                if not last:
                    values(b + 1)
                attend(b)

            over_batches(pe, batch)

            pe.wait_ge(w2t_copied, 1)
            for i in range(FI):
                mm = pe.transpose(w2_ps[:, i * D:(i + 1) * D], w2t[:, i * P:(i + 1) * P], ident[:, :])
            mm.then_inc(w2_ready, 1)

            def ff_in(g, i):
                pe.matmul(h_ps[i], w1[:, i, :], x1T[:, bass.ds(g * GT * P, GT * P)],
                          start=True, stop=True).then_inc(h_ready, 1)

            def ff_out(g, i):
                pe.wait_ge(h_done, FI * g + i + 1)
                for t in range(GT):
                    mm = pe.matmul(ff_ps[:, t * D:(t + 1) * D], hT[:, i, t * P:(t + 1) * P], w2[:, i, :],
                                   start=(i == 0 and t == 0), stop=(i == FI - 1), skip_group_check=True)
                return mm

            for i in range(FI):
                ff_in(0, i)
                if i == 1:
                    turn_x1(B - 2)
            project_out(B - 1)
            pe.wait_ge(w2_copied, 1)
            for i in range(FI):
                mm = ff_out(0, i)
            mm.then_inc(ff_ready, 1)

            def group(g, second=False):
                for i in range(FI):
                    ff_in(g, i)
                    if i == 1:
                        pe.wait_ge(zz_made, g)
                    if i >= 1:
                        ff_out(g, i - 1)
                if second:
                    turn_x1(B - 1)
                ff_out(g, FI - 1).then_inc(ff_ready, 1)

            group(1, second=True)
            pe.wait_ge(x1T_copied, B)
            with pe.Fori(2, GROUPS) as g:
                group(g)

        @block.scalar
        def _(act):
            act.dma_start(bqkv[:, :], b_qkv).then_inc(biases_loaded, 16)
            act.dma_start(qm[:, :], qmask).then_inc(biases_loaded, 16)
            act.wait_ge(xT_cleared, 1)
            act.activation(warm[:, :], xT[:, 0:1], ACT.Exp).then_inc(warmed, 1)
            act.dma_start(ident[:, :], eye).then_inc(ident_loaded, 16)
            act.dma_start(bout[:, :], b_out.rearrange("(a n) -> a n", a=1).broadcast_to([P, D]))\
               .then_inc(bout_loaded, 16)
            act.dma_start(lg[:, 0, :], lg1.rearrange("(a n) -> a n", a=1).broadcast_to([P, NP]))\
               .then_inc(logits_loaded, 16)
            act.dma_start(lg[:, 1, :], lg2.rearrange("(a n) -> a n", a=1).broadcast_to([P, NP]))\
               .then_inc(logits_loaded, 16)

            def place_qk(b):
                act.wait_ge(qk_ready, b + 1)
                for u in range(NQ):
                    act.activation(qx[:, :, u, :], qk_ps[:, 0:S].rearrange("p (m q) -> p m q", q=QB), ACT.Identity, bias=bqm[:, u:u + 1],
                                   scale=qm[:, u:u + 1]).then_inc(qk_placed, 1)
                for j in range(NQ):
                    r = slice(QB * j, QB * (j + 1))
                    act.activation(kx[r, j, HALO:HALO + S], qk_ps[r, S:2 * S], ACT.Identity,
                                   bias=bqkv[r, 1:2]).then_inc(qk_placed, 1)

            def place_v(b):
                act.wait_ge(v_ready, b + 1)
                for u in range(NQ):
                    r = slice(QB * u, QB * (u + 1))
                    act.activation(vx[r, :, :, u, 0:HD],
                                   v_ps[r, :].rearrange("p (m j d) -> p m j d", m=NWIN, j=NQ),
                                   ACT.Copy).then_inc(v_placed, 1)

            def exponentials(b, u):
                act.wait_ge(shifted, 2 * b + u + 1)
                act.activation(pr[:, u, :, 0:KW], pr[:, u, :, 0:KW], ACT.Exp).then_inc(exp_done, 1)

            def copy_x1T(b):
                act.wait_ge(x1_turned, b + 1)
                act.activation(x1T[:, bass.ds(b * S, S)], yt_ps, ACT.Copy).then_inc(x1T_copied, 1)

            act.wait_ge(cleared, 3)
            act.wait_ge(bqm_made, 1)
            place_qk(0)
            act.wait_ge(vx_cleared, 5)
            place_v(0)

            act.wait_ge(lg_step, 2)
            act.activation(lexp[:, :, :], lsh[:, :, :], ACT.Exp).then_inc(lg_exp, 1)

            def batch(b, first=False, mid=False, last=False):
                if mid:
                    act.wait_ge(composed, MID)
                    act.activation(w1[:, :, :].rearrange("p i q -> p (i q)"), w_ps, ACT.Copy).then_inc(w1_copied, 1)
                exponentials(b, 0)
                if not (isinstance(b, int) and b < 2):
                    copy_x1T(b - 2)
                exponentials(b, 1)
                if not last:
                    place_qk(b + 1)
                    act.wait_ge(normalised, b + 1)
                    place_v(b + 1)

            over_batches(act, batch)
            act.wait_ge(composed, B)
            act.activation(w2t[:, :], w_ps, ACT.Copy).then_inc(w2t_copied, 1)
            act.wait_ge(w2_ready, 1)
            act.activation(w2[:, :, :].rearrange("p i d -> p (i d)"), w2_ps, ACT.Copy).then_inc(w2_copied, 1)
            copy_x1T(B - 2)

            def gelu(g, first=False):
                for i in range(FI):
                    act.wait_ge(h_ready, FI * g + i + 1)
                    if i == 0 and not first:
                        act.wait_ge(ff_ready, g)
                    act.activation(hT[:, i, :], h_ps[i], ACT.Gelu_apprx_tanh).then_inc(h_done, 1)

            gelu(0, first=True)
            gelu(1)
            copy_x1T(B - 1)
            with act.Fori(2, GROUPS) as g:
                gelu(g)

        @block.vector
        def _(dve):
            dve.memset(xT[:, :], 0.0).then_inc(xT_cleared, 1)
            dve.memset(kx[:, :, :], 0.0).then_inc(cleared, 1)
            dve.memset(pr[:, 0, :, KW:], 0.0).then_inc(cleared, 1)
            dve.memset(pr[:, 1, :, KW:], 0.0).then_inc(cleared, 1)
            dve.wait_ge(vx_cleared, 1)
            for u in range(NQ):
                dve.memset(vx[QB * u:QB * (u + 1), :, :, u, HD], 1.0).then_inc(vx_cleared, 1)
            dve.wait_ge(biases_loaded, 32)
            dve.tensor_scalar(bqm[:, :], qm[:, :], bqkv[:, 0:1], None, ALU.mult).then_inc(bqm_made, 1)
            dve.wait_ge(band_loaded, 16)
            dve.tensor_copy(band_bf[:, :, :, :], band_f[:, :, :].unsqueeze(2).broadcast_to([P, 3, NQ, KW]))\
               .then_inc(consts_made, 1)
            dve.wait_ge(ident_loaded, 16)
            dve.tensor_copy(ident_bf[:, :], ident[:, :]).then_inc(consts_made, 1)
            dve.wait_ge(bout_loaded, 16)
            dve.wait_ge(rowb_ready, 1)
            dve.tensor_tensor(row_bias[:, :], ps[:, 0, 0:D], bout[:, :], ALU.add).then_inc(rowb_made, 1)

            def shift(b, u):
                s4 = scores_ps(u).rearrange("p c (g k) -> p c g k", k=KW)
                t3 = top[:, u, :].rearrange("p (c g) -> p c g", c=2)
                for c in range(2):
                    dve.wait_ge(scored, 4 * b + 2 * u + c + 1)
                    dve.tensor_reduce(t3[:, c, :], s4[:, c, :, :], AX.X, ALU.max).then_inc(max_found, 1)
                dve.wait_ge(max_found, 4 * b + 2 * u + 2)
                dve.tensor_tensor(pr[:, u, :, 0:KW].rearrange("p (c g) k -> p c g k", c=2), s4,
                                  t3.unsqueeze(3).broadcast_to([P, 2, HALF * NQ // 2, KW]),
                                  ALU.subtract).then_inc(shifted, 1)

            def add_residual(b):
                dve.wait_ge(y_ready, b + 1)
                dve.wait_ge(x_biased, b + 1)
                if not (isinstance(b, int) and b == 0):
                    dve.wait_ge(x1_made, 2 * b)
                dve.tensor_tensor(z[:, :, :], yt_ps.rearrange("p (t d) -> p t d", t=TILES),
                                  xr[:, bass.ds(b * TILES, TILES), :], ALU.add).then_inc(z_added, 1)
                dve.wait_ge(z_added, b + 1)
                for t in range(TILES):
                    dve.bn_stats(stats[:, t, :], z[:, t, :]).then_inc(stats_made, 1)

            def moments(b):
                for t in range(TILES):
                    dve.bn_aggr(mv[:, t, :], stats[:, t, :]).then_inc(mv_made, 1)

            def turn_p(b, u, blocks=slice(0, HALF)):
                g = slice(blocks.start * NQ, blocks.stop * NQ)
                dve.wait_ge(exp_done, 2 * b + u + 1)
                dve.transpose(pT[:, u, blocks, :, :, :].rearrange("p n j w q -> p (n j w q)"),
                              pr[:, u, g, :].rearrange("p g k -> p (g k)")).then_inc(p_turned, 1)

            def normalise(b):
                c3 = cx_ps.rearrange("p a (g e) -> p a g e", e=HD + 1)
                dve.wait_ge(attended, b + 1)
                dve.reciprocal(rden[:, :].rearrange("p (a g) -> p a g", a=2), c3[:, :, :, HD]).then_inc(den_inverted, 1)
                dve.wait_ge(den_inverted, b + 1)
                dve.tensor_tensor(cx[:, :, :].rearrange("p (a m) (u d) -> p a (m u) d", a=2, u=NQ), c3[:, :, :, 0:HD],
                                  rden[:, :].rearrange("p (a g) -> p a g", a=2).unsqueeze(3)
                                  .broadcast_to([P, 2, HALF * NQ, HD]),
                                  ALU.mult).then_inc(normalised, 1)
                dve.wait_ge(normalised, b + 1)
                dve.transpose(cT[:, :, :].rearrange("p m q -> p (m q)"),
                              cx[:, :, :].rearrange("p m e -> p (m e)")).then_inc(cx_turned, 1)

            def batch(b, first=False, mid=False, last=False):
                shift(b, 0)
                shift(b, 1)
                turn_p(b, 0)
                turn_p(b, 1, slice(0, HALF // 2))
                if not first:
                    add_residual(b - 1)
                    dve.wait_ge(stats_made, TILES * b)
                turn_p(b, 1, slice(HALF // 2, HALF))
                if not first:
                    moments(b - 1)
                normalise(b)

            dve.wait_ge(logits_loaded, 32)
            dve.tensor_reduce(lmax[:, :], lg[:, :, :], AX.X, ALU.max).then_inc(lg_step, 1)
            dve.wait_ge(lg_step, 1)
            dve.tensor_tensor(lsh[:, :, :], lg[:, :, :], lmax[:, :].unsqueeze(2).broadcast_to([P, 2, NP]),
                              ALU.subtract).then_inc(lg_step, 1)
            dve.wait_ge(lg_exp, 1)
            dve.tensor_reduce(lsum[:, :], lexp[:, :, :], AX.X, ALU.add).then_inc(lg_step, 1)
            dve.wait_ge(lg_step, 3)
            dve.reciprocal(linv[:, :], lsum[:, :]).then_inc(lg_step, 1)
            dve.wait_ge(lg_step, 4)
            for k in range(KK):
                r = slice(R * k, R * (k + 1))
                for n in range(2):
                    dve.tensor_scalar(wcol[r, n * CH:(n + 1) * CH], lexp[r, n, k::KK], linv[r, n:n + 1], None,
                                      ALU.mult).then_inc(wcol_made, 1)

            over_batches(dve, batch)
            add_residual(B - 1)
            dve.wait_ge(stats_made, TILES * B)
            moments(B - 1)

            def finish(g, first=False):
                dve.wait_ge(ff_ready, g + 1)
                if first:
                    dve.wait_ge(x1_kept, B)
                else:
                    dve.wait_ge(yo_made, GT * g)
                dve.tensor_tensor(zz[:, :, :], ff_ps.rearrange("p (t d) -> p t d", t=GT),
                                  x1_all[:, bass.ds(g * GT, GT), :], ALU.add).then_inc(zz_made, 1)
                dve.wait_ge(zz_made, g + 1)
                for t in range(GT):
                    dve.bn_stats(stats2[:, t, :], zz[:, t, :]).then_inc(stats2_made, 1)
                dve.wait_ge(stats2_made, GT * (g + 1))
                for t in range(GT):
                    dve.bn_aggr(mv2[:, t, :], stats2[:, t, :]).then_inc(mv2_made, 1)
                if not first:
                    dve.wait_ge(stored, 16 * g)
                dve.wait_ge(rstd2_made, 2 * g + 2)
                for t in range(GT):
                    dve.tensor_scalar(yo[:, t, :], zz[:, t, :], mv2[:, t, 0:1], rstd2[:, t:t + 1],
                                      ALU.subtract, ALU.mult).then_inc(yo_made, 1)

            for g in range(GROUPS):
                finish(g, first=(g == 0))

        @block.gpsimd
        def _(pool):
            pool.memset(vx[:, :, :, :, :], 0.0).then_inc(vx_cleared, 1)
            pool.memset(epsc[:, :], EPS).then_inc(rstd_made, 1)
            pool.memset(halfc[:, :], -0.5).then_inc(rstd_made, 1)
            pool.wait_ge(rowb_made, 1)
            pool.wait_ge(resid_loaded, 16)

            def bias_x(b):
                xb = xr[:, bass.ds(b * TILES, TILES), :]
                pool.tensor_tensor(xb, xb,
                                   row_bias[:, :].unsqueeze(1).broadcast_to([P, TILES, D]),
                                   ALU.add).then_inc(x_biased, 1)

            def scale_parts(b):
                pool.wait_ge(parts_loaded[0], 16 * (b + 1))
                if not (isinstance(b, int) and b == 0):
                    pool.wait_ge(composed, b)
                cs = bass.ds(b * CB, CB)
                pool.tensor_tensor(narw[:, :, :], nar[:, cs, :],
                                   wcol[:, cs].unsqueeze(2).broadcast_to([P, CB, D]),
                                   ALU.mult).then_inc(narrow_scaled, 1)

            def normalise_z(b, first=False):
                pool.wait_ge(mv_made, TILES * (b + 1))
                pool.tensor_tensor(rstd[:, :], mv[:, :, 1], epsc[:, 0:TILES], ALU.add).then_inc(rstd_made, 1)
                pool.wait_ge(rstd_made, 2 * b + 3)
                pool.tensor_tensor(rstd[:, :], rstd[:, :], halfc[:, 0:TILES], ALU.pow).then_inc(rstd_made, 1)
                pool.wait_ge(rstd_made, 2 * b + 4)
                if not first:
                    pool.wait_ge(x1_turned, b)
                    pool.wait_ge(x1_kept, b)
                pool.tensor_tensor(x1[:, :, :], z[:, :, :], mv[:, :, 0:1].broadcast_to([P, TILES, D]),
                                   ALU.subtract).then_inc(x1_made, 1)
                pool.wait_ge(x1_made, 2 * b + 1)
                pool.tensor_tensor(x1[:, :, :], x1[:, :, :], rstd[:, :].unsqueeze(2).broadcast_to([P, TILES, D]),
                                   ALU.mult).then_inc(x1_made, 1)
                pool.wait_ge(x1_made, 2 * b + 2)
                pool.tensor_copy(x1_all[:, bass.ds(b * TILES, TILES), :], x1[:, :, :]).then_inc(x1_kept, 1)

            bias_x(0)
            bias_x(1)
            pool.wait_ge(wcol_made, 4)
            scale_parts(0)
            scale_parts(1)
            normalise_z(0, first=True)
            with pool.Fori(1, B - 1) as b:
                bias_x(b + 1)
                scale_parts(b + 1)
                normalise_z(b)
            normalise_z(B - 1)

            with pool.Fori(0, GROUPS) as g:
                pool.wait_ge(mv2_made, GT * (g + 1))
                pool.tensor_tensor(rstd2[:, :], mv2[:, :, 1], epsc[:, :], ALU.add).then_inc(rstd2_made, 1)
                pool.wait_ge(rstd2_made, 2 * g + 1)
                pool.tensor_tensor(rstd2[:, :], rstd2[:, :], halfc[:, :], ALU.pow).then_inc(rstd2_made, 1)


def shape_constants():
    import numpy as np

    eye = np.eye(P, dtype=np.float32)
    r = np.arange(P)[:, None] % QB
    w = np.arange(KW)[None, :]
    band = np.stack([(w >= r) & (w <= r + WIN) & (w >= HALO),
                     (w >= r) & (w <= r + WIN),
                     (w >= r) & (w <= r + WIN) & (w < KW - HALO)], axis=1)
    band = np.where(band, 0.0, -1e30).astype(np.float32)
    qmask = ((np.arange(P)[:, None] // HD) % NQ == np.arange(NQ)[None, :]) * SCALE
    return eye, band, qmask.astype(np.float32)


def kernel(**inputs):
    import numpy as np
    import concourse.bacc as bacc
    from concourse.bass_utils import run_bass_kernel_spmd

    eye, band, qmask = shape_constants()
    x = np.asarray(inputs["L0_attn_input_embeddings"])
    w_qkv = np.asarray(inputs["L0_attn_w_qkv"])
    rows = {
        "x": x,
        "x_t": x.transpose(2, 0, 1),
        "w_qk_t": w_qkv[:2 * D].T,
        "w_v_t": w_qkv[2 * D:].T.reshape(D, NQ, NQ, HD).transpose(0, 2, 1, 3).reshape(D, D),
        "b_qkv": np.asarray(inputs["L0_attn_b_qkv"]).reshape(3, D).T,
        "w_out_t": np.asarray(inputs["L0_attn_w_out"]).T,
        "b_out": np.asarray(inputs["L0_attn_b_out"]),
        "narrow": np.concatenate([np.asarray(inputs["L0_ffn_fc1_A"]).transpose(0, 2, 1).reshape(NP * R, D),
                                  np.asarray(inputs["L0_ffn_fc2_B"]).reshape(NP * R, D)]),
        "wide": np.concatenate([np.asarray(inputs["L0_ffn_fc1_B"]).reshape(NP * R, F),
                                np.asarray(inputs["L0_ffn_fc2_A"]).transpose(0, 2, 1).reshape(NP * R, F)]),
        "fc1_logits": np.asarray(inputs["L0_ffn_fc1_logits"]),
        "fc2_logits": np.asarray(inputs["L0_ffn_fc2_logits"]),
    }
    arrays = {"in_" + n: np.ascontiguousarray(a) for n, a in rows.items()}
    arrays.update(c_eye=eye, c_band=band, c_qmask=qmask)
    nc = bacc.Bacc("TRN2", target_bir_lowering=False, num_devices=1)
    args = [nc.dram_tensor(n, a.shape, F32, kind="ExternalInput").ap() for n, a in arrays.items()]
    out = nc.dram_tensor("out", (B, S, D), F32, kind="ExternalOutput").ap()
    block_kernel(nc, *args, out)
    r = run_bass_kernel_spmd(nc, [arrays], core_ids=[0])
    return r.results[0]["out"]
```

```python
from contextlib import ExitStack

import concourse.bass as bass
from concourse import mybir

F32 = mybir.dt.float32
F32R = mybir.dt.float32r
BF16 = mybir.dt.bfloat16
ALU = mybir.AluOpType
ACT = mybir.ActivationFunctionType
AX = mybir.AxisListType

P = 128
B, S, D = 8, 256, 128
H, HD = 16, 8
WIN = 16
HALO = WIN // 2
QB = 32
KW = QB + WIN
NQ = 4
BLOCKS = S // QB
HALF = BLOCKS // 2
NWIN = BLOCKS + 1
XW = NWIN * QB
TILES = S // P
F = 512
FI = F // P
NP, R = 32, 64
CH = NP * R // P
CB = 2 * CH // B
WARM = 8
RING = 4
MID = CH // CB
KK = P // R
GT = 4
GROUPS = B * TILES // GT
EPS = 1e-5
SCALE = float(HD) ** -0.5


def block_kernel(nc, x, xt, w_qk_t, w_v_t, b_qkv, w_out_t, b_out, narrow, wide, lg1, lg2, eye, band, qmask, out):
    x_v = x.rearrange("b (t p) d -> p (b t) d", p=P)
    out_v = out.rearrange("b (t p) d -> p (b t) d", p=P)
    narrow_v = narrow.rearrange("(c p) d -> p c d", p=P)
    wide_v = wide.rearrange("(c p) f -> p c f", p=P)

    with ExitStack() as ctx:
        def sb(name, shape, dt=F32):
            return ctx.enter_context(nc.sbuf_tensor(name, shape, dt))

        def sem(name):
            return ctx.enter_context(nc.semaphore(name))

        ident = sb("ident", [P, P])
        ident_bf = sb("ident_bf", [P, P], BF16)
        band_f = sb("band_f", [P, 3, KW])
        band_bf = sb("band_bf", [P, 3, NQ, KW], BF16)
        qm = sb("qm", [P, NQ])
        wqkT = sb("wqkT", [P, 2, D])
        wvT = sb("wvT", [P, NQ, NQ * HD])
        woutT = sb("woutT", [P, D])
        bqkv = sb("bqkv", [P, 3])
        bqm = sb("bqm", [P, NQ])
        bout = sb("bout", [P, D])
        row_bias = sb("row_bias", [P, D])
        xT = sb("xT", [P, XW])
        qx = sb("qx", [P, BLOCKS, NQ, QB])
        kx = sb("kx", [P, NQ, S + WIN])
        vx = sb("vx", [P, NWIN, NQ, NQ, HD + 1])
        top = sb("top", [P, 2, HALF * NQ])
        pr = sb("pr", [P, 2, HALF * NQ, 2 * QB])
        pT = sb("pT", [P, 2, HALF, NQ, 2, QB])
        rden = sb("rden", [P, BLOCKS * NQ])
        cx = sb("cx", [P, BLOCKS, NQ * HD])
        cT = sb("cT", [P, BLOCKS, QB])
        z = sb("z", [P, TILES, D])
        stats = sb("stats", [P, TILES, 6])
        mv = sb("mv", [P, TILES, 2])
        rstd = sb("rstd", [P, TILES])
        x1 = sb("x1", [P, TILES, D])
        xr = sb("xr", [P, B * TILES, D])
        x1_all = sb("x1_all", [P, B * TILES, D])
        x1h = sb("x1h", [P, B * S], F32R)
        x1l = sb("x1l", [P, B * S], F32R)
        lg = sb("lg", [P, 2, NP])
        lmax = sb("lmax", [P, 2])
        lsh = sb("lsh", [P, 2, NP])
        lexp = sb("lexp", [P, 2, NP])
        lsum = sb("lsum", [P, 2])
        linv = sb("linv", [P, 2])
        wcol = sb("wcol", [P, 2 * CH])
        nar = sb("nar", [P, 2 * CH, D])
        narw = sb("narw", [P, CB, D])
        wid = sb("wid", [P, RING, CB, F])
        narh = sb("narh", [P, CB, D], F32R)
        narl = sb("narl", [P, CB, D], F32R)
        widh = sb("widh", [P, 2, CB, F], F32R)
        widl = sb("widl", [P, 2, CB, F], F32R)
        w1h = sb("w1h", [P, F], F32R)
        w1l = sb("w1l", [P, F], F32R)
        w2t = sb("w2t", [P, F])
        w2 = sb("w2", [P, FI, D])
        hT = sb("hT", [P, FI, GT * P])
        zz = sb("zz", [P, GT, D])
        stats2 = sb("stats2", [P, GT, 6])
        mv2 = sb("mv2", [P, GT, 2])
        rstd2 = sb("rstd2", [P, GT])
        yo = sb("yo", [P, 2, GT, D])
        warm = sb("warm", [P, 1])
        warm_in = sb("warm_in", [P, 512], BF16)
        epsc = sb("epsc", [P, GT])
        halfc = sb("halfc", [P, GT])
        ps = ctx.enter_context(nc.psum_tensor("ps", [P, 8, 512], F32))

        def scores_ps(u):
            return ps[:, 2 * u:2 * u + 2, 0:2 * NQ * KW]
        q_ps = ps[:, 4, 0:S]

        def k_ps(first):
            return ps[:, 7, 0:S] if first else ps[:, 4, S:2 * S]
        yt_ps = ps[:, 5, 0:S]
        v_cols = NWIN * NQ * HD
        v_ps = ps[:, 6, 0:v_cols]
        cx_ps = ps[:, 5:7, v_cols:v_cols + HALF * NQ * (HD + 1)]
        w_ps = ps[:, 7, :]
        y_last_ps = ps[:, 7, 0:S]
        w2_ps = ps[:, 4, :]
        h_ps = [ps[:, 0, :], ps[:, 1, :], ps[:, 2, :], ps[:, 3, :]]
        ff_ps = ps[:, 6, :]
        fl_ps = [ps[:, 4 + t, 0:D] for t in range(GT)]

        x_loaded = sem("x_loaded")
        wqk_loaded = sem("wqk_loaded")
        wv_loaded = sem("wv_loaded")
        wout_loaded = sem("wout_loaded")
        resid_loaded = sem("resid_loaded")
        ident_loaded = sem("ident_loaded")
        band_loaded = sem("band_loaded")
        biases_loaded = sem("biases_loaded")
        logits_loaded = sem("logits_loaded")
        bout_loaded = sem("bout_loaded")
        parts_loaded = [sem(f"parts_loaded{n}") for n in range(2)]
        stored = [sem(f"stored{n}") for n in range(2)]

        xT_cleared = sem("xT_cleared")
        cleared = sem("cleared")
        vx_cleared = sem("vx_cleared")
        consts_made = sem("consts_made")
        warmed = sem("warmed")
        warm_made = sem("warm_made")
        bqm_made = sem("bqm_made")
        rowb_ready = sem("rowb_ready")
        rowb_made = sem("rowb_made")
        lg_step = sem("lg_step")
        lg_exp = sem("lg_exp")
        wcol_made = sem("wcol_made")

        x_biased = sem("x_biased")
        qk_ready = sem("qk_ready")
        qk_placed = sem("qk_placed")
        v_ready = sem("v_ready")
        v_placed = sem("v_placed")
        scored = sem("scored")
        max_found = sem("max_found")
        shifted = sem("shifted")
        exp_done = sem("exp_done")
        p_turned = sem("p_turned")
        attended = sem("attended")
        den_inverted = sem("den_inverted")
        normalised = sem("normalised")
        cx_turned = sem("cx_turned")
        y_ready = sem("y_ready")
        z_added = sem("z_added")
        stats_made = sem("stats_made")
        mv_made = sem("mv_made")
        rstd_made = sem("rstd_made")
        x1_made = sem("x1_made")
        x1_kept = sem("x1_kept")
        x1_turned = sem("x1_turned")
        x1T_copied = sem("x1T_copied")
        x1T_split = sem("x1T_split")

        narrow_scaled = sem("narrow_scaled")
        narrow_high = sem("narrow_high")
        narrow_low = sem("narrow_low")
        wide_high = [sem(f"wide_high{n}") for n in range(2)]
        wide_low = [sem(f"wide_low{n}") for n in range(2)]
        composed = sem("composed")
        w1_copied = sem("w1_copied")
        w1_split = sem("w1_split")
        w2t_copied = sem("w2t_copied")
        w2_ready = sem("w2_ready")
        w2_copied = sem("w2_copied")
        h_ready = sem("h_ready")
        h_done = sem("h_done")
        ff_ready = sem("ff_ready")
        tile_ready = sem("tile_ready")
        zz_made = sem("zz_made")
        stats2_made = sem("stats2_made")
        mv2_made = sem("mv2_made")
        rstd2_made = sem("rstd2_made")
        yo_made = sem("yo_made")

        block = ctx.enter_context(nc.Block())

        WH = CB // 2

        def wide(t, b, n):
            return t[:, bass.ds(b % 2, 1), n * WH:(n + 1) * WH, :].rearrange("p a c f -> p (a c f)")

        def wide_loaded(b, n):
            return wid[:, bass.ds(b % RING, 1), n * WH:(n + 1) * WH, :].rearrange("p a c f -> p (a c f)")

        def over_batches(eng, batch):
            batch(0, first=True)
            batch(1)
            with eng.Fori(2, MID) as b:
                batch(b)
            batch(MID, mid=True)
            with eng.Fori(MID + 1, B - 1) as b:
                batch(b)
            batch(B - 1, last=True)

        @block.sync
        def _(sp):
            sp.dma_start(wqkT[:, :, :], w_qk_t.rearrange("d (n m) -> d n m", n=2)).then_inc(wqk_loaded, 16)
            sp.dma_start(xT[:, HALO:HALO + S], xt[:, 0, :]).then_inc(x_loaded, 16)
            sp.dma_start(wvT[:, :, :], w_v_t.rearrange("d (u e) -> d u e", u=NQ)).then_inc(wv_loaded, 16)
            sp.dma_start(band_f[:, :, :], band).then_inc(band_loaded, 16)
            sp.dma_start(woutT[:, :], w_out_t).then_inc(wout_loaded, 16)

            def load_parts(b):
                cs = bass.ds(b * CB, CB)
                if not (isinstance(b, int) and b == 0):
                    for n in range(2):
                        sp.wait_ge(parts_loaded[n], 16 * b)
                sp.dma_start(nar[:, cs, :], narrow_v[:, cs, :]).then_inc(parts_loaded[0], 16)
                sp.dma_start(wid[:, bass.ds(b % RING, 1), :, :].rearrange("p a c f -> p (a c) f"),
                             wide_v[:, cs, :]).then_inc(parts_loaded[1], 16)

            load_parts(0)

            def batch(b):
                sp.wait_ge(v_ready, b + 1)
                sp.dma_start(xT[:, HALO:HALO + S], xt[:, bass.ds(b + 1, 1), :].rearrange("d a s -> d (a s)"))\
                  .then_inc(x_loaded, 16)
                if isinstance(b, int) and b == 0:
                    sp.dma_start(xr[:, :, :], x_v).then_inc(resid_loaded, 16)
                    load_parts(1)
                if not (isinstance(b, int) and b < 2):
                    for n in range(2):
                        sp.wait_ge(wide_low[n], b - 1)
                if not (isinstance(b, int) and b == B - 2):
                    load_parts(b + 2)

            batch(0)
            batch(1)
            with sp.Fori(2, B - 2) as b:
                batch(b)
            batch(B - 2)

            for g in range(GROUPS - 1):
                sp.wait_ge(yo_made, GT * (g + 1))
                sp.dma_start(out_v[:, g * GT:(g + 1) * GT, :], yo[:, g % 2, :, :]).then_inc(stored[g % 2], 16)
            g = GROUPS - 1
            for t in range(0, GT, 2):
                sp.wait_ge(yo_made, GT * g + t + 2)
                sp.dma_start(out_v[:, g * GT + t:g * GT + t + 2, :], yo[:, g % 2, t:t + 2, :])\
                  .then_inc(stored[g % 2], 16)
            sp.wait_ge(stored[0], 16 * GROUPS // 2)
            sp.wait_ge(stored[1], 16 * (GROUPS // 2 + 1))

        @block.tensor
        def _(pe):
            def project(b):
                pe.wait_ge(x_loaded, 16 * (b + 1))
                first = isinstance(b, int) and b == 0
                pe.matmul(k_ps(first), wqkT[:, 1, :], xT[:, HALO:HALO + S], start=True, stop=True).then_inc(qk_ready, 1)
                pe.matmul(q_ps, wqkT[:, 0, :], xT[:, HALO:HALO + S], start=True, stop=True).then_inc(qk_ready, 1)

            def values(b):
                if not (isinstance(b, int) and b == 0):
                    pe.wait_ge(v_placed, NQ * b)
                for m in range(NWIN):
                    for u in range(NQ):
                        mm = pe.matmul(v_ps[QB * u:QB * (u + 1), m * NQ * HD:(m + 1) * NQ * HD],
                                       xT[:, m * QB:(m + 1) * QB], wvT[:, u, :], start=True, stop=True)
                mm.then_inc(v_ready, 1)

            def scores(b):
                pe.wait_ge(qk_placed, 8 * (b + 1))
                for u in range(2):
                    for n in range(HALF):
                        m = u * HALF + n
                        o = scores_ps(u)[:, n // 2, (n % 2) * NQ * KW:(n % 2 + 1) * NQ * KW]
                        kind = 0 if m == 0 else 2 if m == BLOCKS - 1 else 1
                        pe.matmul(o, qx[:, m, :, :], kx[:, :, m * QB:m * QB + KW],
                                  start=True, stop=False)
                        mm = pe.matmul(o, ident_bf[:, :], band_bf[:, kind, :, :], start=False, stop=True)
                        if n % 2 == 1:
                            mm.then_inc(scored, 1)

            def attend(b):
                pe.wait_ge(v_placed, 4 * (b + 1))
                if not (isinstance(b, int) and b == 0):
                    pe.wait_ge(z_added, b)
                else:
                    pe.wait_ge(rowb_made, 1)
                for u in range(2):
                    for n in range(HALF):
                        if n == 0:
                            pe.wait_ge(p_turned, 3 * b + u + 1)
                        if u == 1 and n == 2:
                            pe.wait_ge(p_turned, 3 * b + 3)
                        m = u * HALF + n
                        for j in range(NQ):
                            o = cx_ps[QB * j:QB * (j + 1), u, n * NQ * (HD + 1):(n + 1) * NQ * (HD + 1)]
                            for w in range(2):
                                mm = pe.matmul(o, pT[:, u, n, j, w, :], vx[:, m + w, j, :, :],
                                               start=(w == 0), stop=(w == 1))
                mm.then_inc(attended, 1)

            def project_out(b):
                y_ps = yt_ps
                if isinstance(b, int) and b == B - 1:
                    y_ps = y_last_ps
                elif not (isinstance(b, int) and b == 0):
                    pe.wait_ge(x1T_split, b)
                pe.wait_ge(cx_turned, b + 1)
                for t in range(TILES):
                    mm = pe.matmul(y_ps[:, t * D:(t + 1) * D], cT[:, t * HALF:(t + 1) * HALF, :],
                                   woutT[:, :], start=True, stop=True)
                mm.then_inc(y_ready, 1)

            def turn_x1(b):
                if not (isinstance(b, int) and b == B - 1):
                    pe.wait_ge(normalised, b + 2)
                pe.wait_ge(x1_made, 2 * b + 2)
                for t in range(TILES):
                    mm = pe.transpose(yt_ps[:, t * P:(t + 1) * P], x1[:, t, :], ident[:, :])
                mm.then_inc(x1_turned, 1)

            def compose(b, start=False, stop=False):
                pe.wait_ge(wide_low[0], b + 1)
                pe.wait_ge(wide_low[1], b + 1)
                pe.wait_ge(narrow_low, b + 1)
                for c in range(CB):
                    high = widh[:, bass.ds(b % 2, 1), c, :].rearrange("p a f -> p (a f)")
                    low = widl[:, bass.ds(b % 2, 1), c, :].rearrange("p a f -> p (a f)")
                    pe.matmul(w_ps, narh[:, c, :], high, start=(start and c == 0), stop=False, skip_group_check=True)
                    pe.matmul(w_ps, narh[:, c, :], low, start=False, stop=False, skip_group_check=True)
                    mm = pe.matmul(w_ps, narl[:, c, :], high,
                                   start=False, stop=(stop and c == CB - 1), skip_group_check=True)
                mm.then_inc(composed, 1)

            def ff_in(g, i):
                f = slice(i * P, (i + 1) * P)
                tokens = bass.ds(g * GT * P, GT * P)
                pe.matmul(h_ps[i], w1h[:, f], x1h[:, tokens], start=True, stop=False)
                pe.matmul(h_ps[i], w1h[:, f], x1l[:, tokens], start=False, stop=False)
                pe.matmul(h_ps[i], w1l[:, f], x1h[:, tokens], start=False, stop=True).then_inc(h_ready, 1)

            def keep_warm(bank, count):
                for n in range(count):
                    pe.matmul(ps[:, bank, :], warm_in[:, 0:P], warm_in[:, :], start=True, stop=True)

            pe.wait_ge(warm_made, 1)
            keep_warm(0, WARM)

            pe.wait_ge(wqk_loaded, 16)
            project(0)
            pe.wait_ge(wv_loaded, 16)
            pe.wait_ge(xT_cleared, 2)
            values(0)
            pe.wait_ge(biases_loaded, 32)
            pe.wait_ge(wout_loaded, 16)
            pe.matmul(yt_ps[:, 0:D], bqkv[:, 2:3].broadcast_to([P, P]), woutT[:, :],
                      start=True, stop=True).then_inc(rowb_ready, 1)
            pe.wait_ge(ident_loaded, 16)
            pe.wait_ge(consts_made, 2)
            pe.wait_ge(cleared, 3)

            def batch(b, first=False, mid=False, last=False):
                scores(b)
                if not (isinstance(b, int) and b < 2):
                    turn_x1(b - 2)
                if not last:
                    project(b + 1)
                if mid:
                    pe.wait_ge(w1_split, 1)
                if not first:
                    compose(b, start=mid, stop=last)
                    project_out(b - 1)
                if not last:
                    values(b + 1)
                if first:
                    keep_warm(7, WARM - 2)
                if last:
                    pe.wait_ge(shifted, 2 * b + 1)
                    ff_in(0, 0)
                    ff_in(0, 1)
                attend(b)
                if first:
                    compose(b, start=True)

            over_batches(pe, batch)

            pe.wait_ge(w2t_copied, 1)
            for i in range(FI):
                mm = pe.transpose(w2_ps[:, i * D:(i + 1) * D], w2t[:, i * P:(i + 1) * P], ident[:, :])
            mm.then_inc(w2_ready, 1)

            def ff_out(g, i):
                pe.wait_ge(h_done, FI * g + i + 1)
                for t in range(GT):
                    mm = pe.matmul(ff_ps[:, t * D:(t + 1) * D], hT[:, i, t * P:(t + 1) * P], w2[:, i, :],
                                   start=(i == 0 and t == 0), stop=(i == FI - 1), skip_group_check=True)
                return mm

            def group(g):
                ff_in(g, 0)
                ff_in(g, 1)
                for i in range(2):
                    ff_in(g, i + 2)
                    if i == 0:
                        pe.wait_ge(zz_made, g)
                    ff_out(g, i)
                ff_out(g, 2)
                ff_out(g, 3).then_inc(ff_ready, 1)

            ff_in(0, 2)
            ff_in(0, 3)
            project_out(B - 1)
            turn_x1(B - 2)
            pe.wait_ge(w2_copied, 1)
            for i in range(FI):
                mm = ff_out(0, i)
            mm.then_inc(ff_ready, 1)
            turn_x1(B - 1)
            with pe.Fori(1, GROUPS - 1) as g:
                group(g)

            g = GROUPS - 1
            pe.wait_ge(x1T_split, B)

            def ff_tile(t, i):
                pe.wait_ge(h_done, FI * g + i + 1)
                return pe.matmul(fl_ps[t], hT[:, i, t * P:(t + 1) * P], w2[:, i, :],
                                 start=(i == 0), stop=(i == FI - 1))

            for i in range(FI):
                ff_in(g, i)
            pe.wait_ge(zz_made, g)
            for t in range(GT):
                ff_tile(t, 0)
            for t in range(GT):
                ff_tile(t, 1)
                ff_tile(t, 2)
                ff_tile(t, 3).then_inc(tile_ready, 1)

        @block.scalar
        def _(act):
            act.dma_start(bqkv[:, :], b_qkv).then_inc(biases_loaded, 16)
            act.dma_start(qm[:, :], qmask).then_inc(biases_loaded, 16)
            act.wait_ge(xT_cleared, 1)
            act.activation(warm[:, :], xT[:, 0:1], ACT.Exp).then_inc(warmed, 1)
            act.dma_start(ident[:, :], eye).then_inc(ident_loaded, 16)
            act.dma_start(bout[:, :], b_out.rearrange("(a n) -> a n", a=1).broadcast_to([P, D]))\
               .then_inc(bout_loaded, 16)
            act.dma_start(lg[:, 0, :], lg1.rearrange("(a n) -> a n", a=1).broadcast_to([P, NP]))\
               .then_inc(logits_loaded, 16)
            act.dma_start(lg[:, 1, :], lg2.rearrange("(a n) -> a n", a=1).broadcast_to([P, NP]))\
               .then_inc(logits_loaded, 16)

            def place_qk(b):
                act.wait_ge(qk_ready, 2 * (b + 1))
                for u in range(NQ):
                    act.activation(qx[:, :, u, :], q_ps.rearrange("p (m q) -> p m q", q=QB), ACT.Identity,
                                   bias=bqm[:, u:u + 1],
                                   scale=qm[:, u:u + 1]).then_inc(qk_placed, 1)
                if isinstance(b, int) and b == 0:
                    return
                for j in range(NQ):
                    r = slice(QB * j, QB * (j + 1))
                    act.activation(kx[r, j, HALO:HALO + S], k_ps(False)[r, :], ACT.Identity,
                                   bias=bqkv[r, 1:2]).then_inc(qk_placed, 1)

            def place_v(b):
                act.wait_ge(v_ready, b + 1)
                for u in range(NQ):
                    r = slice(QB * u, QB * (u + 1))
                    act.activation(vx[r, :, :, u, 0:HD],
                                   v_ps[r, :].rearrange("p (m j d) -> p m j d", m=NWIN, j=NQ),
                                   ACT.Copy).then_inc(v_placed, 1)

            def exponentials(b, u):
                act.wait_ge(shifted, 2 * b + u + 1)
                act.activation(pr[:, u, :, 0:KW], pr[:, u, :, 0:KW], ACT.Exp).then_inc(exp_done, 1)

            def copy_x1T(b):
                act.wait_ge(x1_turned, b + 1)
                act.activation(x1h[:, bass.ds(b * S, S)], yt_ps, ACT.Copy).then_inc(x1T_copied, 1)

            def split_wide(b, n):
                act.wait_ge(parts_loaded[1], 16 * (b + 1))
                if not (isinstance(b, int) and b < 2):
                    act.wait_ge(composed, b - 1)
                act.activation(wide(widh, b, n), wide_loaded(b, n), ACT.Copy).then_inc(wide_high[n], 1)

            def split_narrow(b):
                act.wait_ge(narrow_scaled, b + 1)
                if not (isinstance(b, int) and b == 0):
                    act.wait_ge(composed, b)
                act.activation(narh[:, :, :], narw[:, :, :], ACT.Copy).then_inc(narrow_high, 1)

            act.wait_ge(cleared, 3)
            act.wait_ge(bqm_made, 1)
            place_qk(0)
            act.wait_ge(vx_cleared, 5)
            place_v(0)

            act.wait_ge(lg_step, 2)
            act.activation(lexp[:, :, :], lsh[:, :, :], ACT.Exp).then_inc(lg_exp, 1)
            split_wide(0, 1)

            def batch(b, first=False, mid=False, last=False):
                if mid:
                    act.wait_ge(composed, MID)
                    act.activation(w1h[:, :], w_ps, ACT.Copy).then_inc(w1_copied, 1)
                if not (first or last):
                    split_wide(b + 1, 0)
                exponentials(b, 0)
                if not (isinstance(b, int) and b < 2):
                    copy_x1T(b - 2)
                if first:
                    split_narrow(0)
                elif not last:
                    split_wide(b + 1, 1)
                exponentials(b, 1)
                if first:
                    split_wide(0, 0)
                if not last:
                    place_qk(b + 1)
                    if first:
                        split_wide(1, 0)
                        split_wide(1, 1)
                    split_narrow(b + 1)
                    act.wait_ge(normalised, b + 1)
                    place_v(b + 1)

            over_batches(act, batch)
            act.wait_ge(composed, B)
            act.activation(w2t[:, :], w_ps, ACT.Copy).then_inc(w2t_copied, 1)

            def gelu(g, i):
                act.wait_ge(h_ready, FI * g + i + 1)
                act.activation(hT[:, i, :], h_ps[i], ACT.Gelu_apprx_tanh).then_inc(h_done, 1)

            gelu(0, 0)
            gelu(0, 1)
            act.wait_ge(w2_ready, 1)
            act.activation(w2[:, :, :].rearrange("p i d -> p (i d)"), w2_ps, ACT.Copy).then_inc(w2_copied, 1)
            gelu(0, 2)
            copy_x1T(B - 2)
            gelu(0, 3)
            copy_x1T(B - 1)
            with act.Fori(1, GROUPS) as g:
                act.wait_ge(ff_ready, g)
                for i in range(FI):
                    gelu(g, i)

        @block.vector
        def _(dve):
            dve.memset(warm_in[:, :], 0.0).then_inc(warm_made, 1)
            dve.memset(xT[:, 0:HALO], 0.0).then_inc(xT_cleared, 1)
            dve.memset(xT[:, HALO + S:], 0.0).then_inc(xT_cleared, 1)
            dve.memset(kx[:, :, :], 0.0).then_inc(cleared, 1)
            dve.memset(pr[:, 0, :, KW:], 0.0).then_inc(cleared, 1)
            dve.memset(pr[:, 1, :, KW:], 0.0).then_inc(cleared, 1)
            dve.wait_ge(vx_cleared, 1)
            for u in range(NQ):
                dve.memset(vx[QB * u:QB * (u + 1), :, :, u, HD], 1.0).then_inc(vx_cleared, 1)
            dve.wait_ge(biases_loaded, 32)
            dve.tensor_scalar(bqm[:, :], qm[:, :], bqkv[:, 0:1], None, ALU.mult).then_inc(bqm_made, 1)
            dve.wait_ge(qk_ready, 1)
            for j in range(NQ):
                r = slice(QB * j, QB * (j + 1))
                if j == 0:
                    dve.wait_ge(cleared, 1)
                dve.tensor_scalar(kx[r, j, HALO:HALO + S], k_ps(True)[r, :], bqkv[r, 1:2], None,
                                  ALU.add).then_inc(qk_placed, 1)
            dve.wait_ge(bout_loaded, 16)
            dve.wait_ge(rowb_ready, 1)
            dve.tensor_tensor(row_bias[:, :], yt_ps[:, 0:D], bout[:, :], ALU.add).then_inc(rowb_made, 1)

            def shift(b, u):
                s4 = scores_ps(u).rearrange("p c (g k) -> p c g k", k=KW)
                t3 = top[:, u, :].rearrange("p (c g) -> p c g", c=2)
                for c in range(2):
                    dve.wait_ge(scored, 4 * b + 2 * u + c + 1)
                    dve.tensor_reduce(t3[:, c, :], s4[:, c, :, :], AX.X, ALU.max).then_inc(max_found, 1)
                dve.wait_ge(max_found, 4 * b + 2 * u + 2)
                dve.tensor_tensor(pr[:, u, :, 0:KW].rearrange("p (c g) k -> p c g k", c=2), s4,
                                  t3.unsqueeze(3).broadcast_to([P, 2, HALF * NQ // 2, KW]),
                                  ALU.subtract).then_inc(shifted, 1)

            def add_residual(b):
                dve.wait_ge(y_ready, b + 1)
                dve.wait_ge(x_biased, b + 1)
                if not (isinstance(b, int) and b == 0):
                    dve.wait_ge(x1_made, 2 * b)
                y_ps = y_last_ps if isinstance(b, int) and b == B - 1 else yt_ps
                dve.tensor_tensor(z[:, :, :], y_ps.rearrange("p (t d) -> p t d", t=TILES),
                                  xr[:, bass.ds(b * TILES, TILES), :], ALU.add).then_inc(z_added, 1)
                dve.wait_ge(z_added, b + 1)
                for t in range(TILES):
                    dve.bn_stats(stats[:, t, :], z[:, t, :]).then_inc(stats_made, 1)

            def split_x1T(b):
                dve.wait_ge(x1T_copied, b + 1)
                s_ = bass.ds(b * S, S)
                dve.tensor_tensor(x1l[:, s_], yt_ps, x1h[:, s_], ALU.subtract).then_inc(x1T_split, 1)

            def split_wide(b):
                dve.wait_ge(wide_high[0], b + 1)
                dve.tensor_tensor(wide(widl, b, 0), wide_loaded(b, 0), wide(widh, b, 0),
                                  ALU.subtract).then_inc(wide_low[0], 1)

            def moments(b):
                for t in range(TILES):
                    dve.bn_aggr(mv[:, t, :], stats[:, t, :]).then_inc(mv_made, 1)

            def turn_p(b, u, blocks=slice(0, HALF)):
                g = slice(blocks.start * NQ, blocks.stop * NQ)
                dve.wait_ge(exp_done, 2 * b + u + 1)
                dve.transpose(pT[:, u, blocks, :, :, :].rearrange("p n j w q -> p (n j w q)"),
                              pr[:, u, g, :].rearrange("p g k -> p (g k)")).then_inc(p_turned, 1)

            def normalise(b):
                c3 = cx_ps.rearrange("p a (g e) -> p a g e", e=HD + 1)
                dve.wait_ge(attended, b + 1)
                dve.reciprocal(rden[:, :].rearrange("p (a g) -> p a g", a=2), c3[:, :, :, HD]).then_inc(den_inverted, 1)
                dve.wait_ge(den_inverted, b + 1)
                dve.tensor_tensor(cx[:, :, :].rearrange("p (a m) (u d) -> p a (m u) d", a=2, u=NQ), c3[:, :, :, 0:HD],
                                  rden[:, :].rearrange("p (a g) -> p a g", a=2).unsqueeze(3)
                                  .broadcast_to([P, 2, HALF * NQ, HD]),
                                  ALU.mult).then_inc(normalised, 1)
                dve.wait_ge(normalised, b + 1)
                dve.transpose(cT[:, :, :].rearrange("p m q -> p (m q)"),
                              cx[:, :, :].rearrange("p m e -> p (m e)")).then_inc(cx_turned, 1)

            def batch(b, first=False, mid=False, last=False):
                shift(b, 0)
                if mid:
                    dve.wait_ge(w1_copied, 1)
                    dve.tensor_tensor(w1l[:, :], w_ps, w1h[:, :], ALU.subtract).then_inc(w1_split, 1)
                shift(b, 1)
                if not (isinstance(b, int) and b < 2):
                    split_x1T(b - 2)
                turn_p(b, 0)
                turn_p(b, 1, slice(0, HALF // 2))
                if not first:
                    add_residual(b - 1)
                    dve.wait_ge(stats_made, TILES * b)
                turn_p(b, 1, slice(HALF // 2, HALF))
                if not first:
                    moments(b - 1)
                if first:
                    split_wide(0)
                elif not last:
                    split_wide(b + 1)
                normalise(b)
                if first:
                    split_wide(1)

            dve.wait_ge(logits_loaded, 32)
            dve.tensor_reduce(lmax[:, :], lg[:, :, :], AX.X, ALU.max).then_inc(lg_step, 1)
            dve.wait_ge(lg_step, 1)
            dve.tensor_tensor(lsh[:, :, :], lg[:, :, :], lmax[:, :].unsqueeze(2).broadcast_to([P, 2, NP]),
                              ALU.subtract).then_inc(lg_step, 1)
            dve.wait_ge(lg_exp, 1)
            dve.tensor_reduce(lsum[:, :], lexp[:, :, :], AX.X, ALU.add).then_inc(lg_step, 1)
            dve.wait_ge(lg_step, 3)
            dve.reciprocal(linv[:, :], lsum[:, :]).then_inc(lg_step, 1)
            dve.wait_ge(lg_step, 4)
            for k in range(KK):
                r = slice(R * k, R * (k + 1))
                for n in range(2):
                    dve.tensor_scalar(wcol[r, n * CH:(n + 1) * CH], lexp[r, n, k::KK], linv[r, n:n + 1], None,
                                      ALU.mult).then_inc(wcol_made, 1)

            over_batches(dve, batch)
            add_residual(B - 1)
            split_x1T(B - 2)
            dve.wait_ge(stats_made, TILES * B)
            moments(B - 1)

            def finish(g, first=False):
                dve.wait_ge(ff_ready, g + 1)
                if first:
                    dve.wait_ge(x1_kept, B)
                else:
                    dve.wait_ge(yo_made, GT * g)
                dve.tensor_tensor(zz[:, :, :], ff_ps.rearrange("p (t d) -> p t d", t=GT),
                                  x1_all[:, bass.ds(g * GT, GT), :], ALU.add).then_inc(zz_made, 1)
                dve.wait_ge(zz_made, g + 1)
                for t in range(GT):
                    dve.bn_stats(stats2[:, t, :], zz[:, t, :]).then_inc(stats2_made, 1)
                dve.wait_ge(stats2_made, GT * (g + 1))
                for t in range(GT):
                    dve.bn_aggr(mv2[:, t, :], stats2[:, t, :]).then_inc(mv2_made, 1)
                if g >= 2:
                    dve.wait_ge(stored[g % 2], 16 * (g // 2))
                dve.wait_ge(rstd2_made, 2 * g + 2)
                for t in range(GT):
                    scale_tile(g, t)

            def scale_tile(g, t):
                dve.tensor_scalar(yo[:, g % 2, t, :], zz[:, t, :], mv2[:, t, 0:1], rstd2[:, t:t + 1],
                                  ALU.subtract, ALU.mult).then_inc(yo_made, 1)

            finish(0, first=True)
            split_x1T(B - 1)
            for g in range(1, GROUPS - 1):
                finish(g)

            g = GROUPS - 1
            dve.wait_ge(yo_made, GT * g)
            for n in range(2):
                pair = (2 * n, 2 * n + 1)
                for t in pair:
                    dve.wait_ge(tile_ready, t + 1)
                    dve.tensor_tensor(zz[:, t, :], fl_ps[t], x1_all[:, g * GT + t, :], ALU.add).then_inc(zz_made, 1)
                for t in pair:
                    dve.wait_ge(zz_made, g + t + 1)
                    dve.bn_stats(stats2[:, t, :], zz[:, t, :]).then_inc(stats2_made, 1)
                for t in pair:
                    dve.wait_ge(stats2_made, GT * g + t + 1)
                    dve.bn_aggr(mv2[:, t, :], stats2[:, t, :]).then_inc(mv2_made, 1)
            dve.wait_ge(stored[g % 2], 16 * (g // 2))
            for n in range(2):
                dve.wait_ge(rstd2_made, 2 * (g + n + 1))
                for t in range(2 * n, 2 * n + 2):
                    scale_tile(g, t)

        @block.gpsimd
        def _(pool):
            pool.memset(vx[:, :, :, :, :], 0.0).then_inc(vx_cleared, 1)
            pool.memset(epsc[:, :], EPS).then_inc(rstd_made, 1)
            pool.memset(halfc[:, :], -0.5).then_inc(rstd_made, 1)
            pool.wait_ge(band_loaded, 16)
            pool.tensor_copy(band_bf[:, :, :, :], band_f[:, :, :].unsqueeze(2).broadcast_to([P, 3, NQ, KW]))\
                .then_inc(consts_made, 1)
            pool.wait_ge(ident_loaded, 16)
            pool.tensor_copy(ident_bf[:, :], ident[:, :]).then_inc(consts_made, 1)

            def bias_x(b):
                xb = xr[:, bass.ds(b * TILES, TILES), :]
                pool.tensor_tensor(xb, xb,
                                   row_bias[:, :].unsqueeze(1).broadcast_to([P, TILES, D]),
                                   ALU.add).then_inc(x_biased, 1)

            def scale_parts(b):
                pool.wait_ge(parts_loaded[0], 16 * (b + 1))
                if not (isinstance(b, int) and b == 0):
                    pool.wait_ge(narrow_low, b)
                cs = bass.ds(b * CB, CB)
                pool.tensor_tensor(narw[:, :, :], nar[:, cs, :],
                                   wcol[:, cs].unsqueeze(2).broadcast_to([P, CB, D]),
                                   ALU.mult).then_inc(narrow_scaled, 1)

            def split_parts(b):
                pool.wait_ge(wide_high[1], b + 1)
                pool.tensor_tensor(wide(widl, b, 1), wide_loaded(b, 1), wide(widh, b, 1),
                                   ALU.subtract).then_inc(wide_low[1], 1)
                pool.wait_ge(narrow_high, b + 1)
                pool.tensor_tensor(narl[:, :, :], narw[:, :, :], narh[:, :, :], ALU.subtract).then_inc(narrow_low, 1)

            def normalise_z(b, first=False):
                pool.wait_ge(mv_made, TILES * (b + 1))
                pool.tensor_tensor(rstd[:, :], mv[:, :, 1], epsc[:, 0:TILES], ALU.add).then_inc(rstd_made, 1)
                pool.wait_ge(rstd_made, 2 * b + 3)
                pool.tensor_tensor(rstd[:, :], rstd[:, :], halfc[:, 0:TILES], ALU.pow).then_inc(rstd_made, 1)
                pool.wait_ge(rstd_made, 2 * b + 4)
                if not first:
                    pool.wait_ge(x1_turned, b)
                    pool.wait_ge(x1_kept, b)
                pool.tensor_tensor(x1[:, :, :], z[:, :, :], mv[:, :, 0:1].broadcast_to([P, TILES, D]),
                                   ALU.subtract).then_inc(x1_made, 1)
                pool.wait_ge(x1_made, 2 * b + 1)
                pool.tensor_tensor(x1[:, :, :], x1[:, :, :], rstd[:, :].unsqueeze(2).broadcast_to([P, TILES, D]),
                                   ALU.mult).then_inc(x1_made, 1)
                pool.wait_ge(x1_made, 2 * b + 2)
                pool.tensor_copy(x1_all[:, bass.ds(b * TILES, TILES), :], x1[:, :, :]).then_inc(x1_kept, 1)

            pool.wait_ge(wcol_made, 4)
            scale_parts(0)
            split_parts(0)
            pool.wait_ge(rowb_made, 1)
            pool.wait_ge(resid_loaded, 16)
            bias_x(0)

            def prepare(b):
                bias_x(b)
                scale_parts(b)
                split_parts(b)

            prepare(1)
            prepare(2)
            normalise_z(0, first=True)
            with pool.Fori(2, B - 1) as b:
                prepare(b + 1)
                normalise_z(b - 1)
            normalise_z(B - 2)
            normalise_z(B - 1)

            with pool.Fori(0, GROUPS - 1) as g:
                pool.wait_ge(mv2_made, GT * (g + 1))
                pool.tensor_tensor(rstd2[:, :], mv2[:, :, 1], epsc[:, :], ALU.add).then_inc(rstd2_made, 1)
                pool.wait_ge(rstd2_made, 2 * g + 1)
                pool.tensor_tensor(rstd2[:, :], rstd2[:, :], halfc[:, :], ALU.pow).then_inc(rstd2_made, 1)
            g = GROUPS - 1
            pool.wait_ge(yo_made, GT * g)
            for n in range(2):
                c = slice(2 * n, 2 * n + 2)
                pool.wait_ge(mv2_made, GT * g + 2 * n + 2)
                pool.tensor_tensor(rstd2[:, c], mv2[:, c, 1], epsc[:, c], ALU.add).then_inc(rstd2_made, 1)
                pool.wait_ge(rstd2_made, 2 * (g + n) + 1)
                pool.tensor_tensor(rstd2[:, c], rstd2[:, c], halfc[:, c], ALU.pow).then_inc(rstd2_made, 1)


def shape_constants():
    import numpy as np

    eye = np.eye(P, dtype=np.float32)
    r = np.arange(P)[:, None] % QB
    w = np.arange(KW)[None, :]
    band = np.stack([(w >= r) & (w <= r + WIN) & (w >= HALO),
                     (w >= r) & (w <= r + WIN),
                     (w >= r) & (w <= r + WIN) & (w < KW - HALO)], axis=1)
    band = np.where(band, 0.0, -1e30).astype(np.float32)
    qmask = ((np.arange(P)[:, None] // HD) % NQ == np.arange(NQ)[None, :]) * SCALE
    return eye, band, qmask.astype(np.float32)


def kernel(**inputs):
    import numpy as np
    import concourse.bacc as bacc
    from concourse.bass_utils import run_bass_kernel_spmd

    eye, band, qmask = shape_constants()
    x = np.asarray(inputs["L0_attn_input_embeddings"])
    w_qkv = np.asarray(inputs["L0_attn_w_qkv"])
    rows = {
        "x": x,
        "x_t": x.transpose(2, 0, 1),
        "w_qk_t": w_qkv[:2 * D].T,
        "w_v_t": w_qkv[2 * D:].T.reshape(D, NQ, NQ, HD).transpose(0, 2, 1, 3).reshape(D, D),
        "b_qkv": np.asarray(inputs["L0_attn_b_qkv"]).reshape(3, D).T,
        "w_out_t": np.asarray(inputs["L0_attn_w_out"]).T,
        "b_out": np.asarray(inputs["L0_attn_b_out"]),
        "narrow": np.concatenate([np.asarray(inputs["L0_ffn_fc1_A"]).transpose(0, 2, 1).reshape(NP * R, D),
                                  np.asarray(inputs["L0_ffn_fc2_B"]).reshape(NP * R, D)]),
        "wide": np.concatenate([np.asarray(inputs["L0_ffn_fc1_B"]).reshape(NP * R, F),
                                np.asarray(inputs["L0_ffn_fc2_A"]).transpose(0, 2, 1).reshape(NP * R, F)]),
        "fc1_logits": np.asarray(inputs["L0_ffn_fc1_logits"]),
        "fc2_logits": np.asarray(inputs["L0_ffn_fc2_logits"]),
    }
    arrays = {"in_" + n: np.ascontiguousarray(a) for n, a in rows.items()}
    arrays.update(c_eye=eye, c_band=band, c_qmask=qmask)
    nc = bacc.Bacc("TRN2", target_bir_lowering=False, num_devices=1)
    args = [nc.dram_tensor(n, a.shape, F32, kind="ExternalInput").ap() for n, a in arrays.items()]
    out = nc.dram_tensor("out", (B, S, D), F32, kind="ExternalOutput").ap()
    block_kernel(nc, *args, out)
    r = run_bass_kernel_spmd(nc, [arrays], core_ids=[0])
    return r.results[0]["out"]
```
